# Optimizing a Trainium2 kernel written in Bass

```python
import numpy as np
import jax
import jax.numpy as jnp

def _softmax(x, axis=-1):
    return jax.nn.softmax(x, axis=axis)

def _gelu(x):
    return jax.nn.gelu(x, approximate=True)

def _silu(x):
    return jax.nn.silu(x)

def _sigmoid(x):
    return jax.nn.sigmoid(x)

def _layernorm(x, axis=-1, eps=1e-05):
    m = jnp.mean(x, axis=axis, keepdims=True)
    v = jnp.var(x, axis=axis, keepdims=True)
    return (x - m) / jnp.sqrt(v + eps)

def _scatter_add(tgt, idx, src, axis=0):
    return tgt.at[idx].add(src)

def _segment_sum(src, seg, n):
    return jax.ops.segment_sum(src, seg, n)
kernel_name = 'mk_adj_preln_d4_adj_r2_de08dc'

def setup_inputs(seed: int=0):
    np.random.seed(seed)
    _w = jnp.asarray

    def _rec_inputs():
        import jax
        import jax.numpy as jnp
        _gk = jax.random.key(seed)
        x = -0.0003929 + 0.9999 * jax.random.normal(jax.random.fold_in(_gk, 1), (8, 1024, 256), jnp.float32)
        _a = jax.random.bernoulli(jax.random.fold_in(_gk, 2), 0.015625, (1024, 1024))
        _a = jnp.logical_or(_a, jnp.swapaxes(_a, -1, -2))
        _a = jnp.logical_or(_a, jnp.eye(1024, dtype=bool))
        _af = _a.astype(jnp.float32)
        _af = _af * jax.random.uniform(jax.random.fold_in(_gk, 3), (1024, 1024), jnp.float32, 0.05, 1)
        adj = _af
        return (x, adj)
    x, adj = _rec_inputs()

    def _L0_gnn_setup():
        import jax, jax.numpy as jnp
        import numpy as np
        B, N, D, O = (8, 2048, 256, 256)
        key = jax.random.key(seed)
        k1, k2, k3, k4 = jax.random.split(key, 4)
        x = jax.random.normal(k1, (B, N, D), dtype=jnp.float32)
        adj = jax.random.uniform(k2, (N, N), dtype=jnp.float32)
        weight = jax.random.normal(k3, (D, O), dtype=jnp.float32) * 0.02
        bias = jax.random.normal(k4, (O,), dtype=jnp.float32) * 0.02
        return {'x': x, 'adj': adj, 'weight': weight, 'bias': bias}
    _L0_gnn_all = _L0_gnn_setup()
    _L0_gnn_in = {k: v for k, v in _L0_gnn_all.items() if k in ('weight', 'bias')}
    del _L0_gnn_all

    def _L1_gnn_setup():
        import jax, jax.numpy as jnp
        import numpy as np
        B, N, F_IN, F_OUT = (16, 1024, 256, 256)
        key = jax.random.key(seed)
        k1, k2, k3 = jax.random.split(key, 3)
        x = jax.random.normal(k1, (B, N, F_IN), dtype=jnp.float32)
        adj = jax.random.uniform(k2, (N, N), dtype=jnp.float32)
        bound = np.sqrt(6.0 / F_OUT)
        weight = jax.random.uniform(k3, (F_IN, F_OUT), dtype=jnp.float32, minval=-bound, maxval=bound)
        bias = jnp.zeros((F_OUT,), dtype=jnp.float32)
        return {'x': x, 'adj': adj, 'weight': weight, 'bias': bias}
    _L1_gnn_all = _L1_gnn_setup()
    _L1_gnn_in = {k: v for k, v in _L1_gnn_all.items() if k in ('weight', 'bias')}
    del _L1_gnn_all

    def _L2_gnn_setup():
        import jax, jax.numpy as jnp
        import numpy as np
        B, N, D, H = (16, 1025, 256, 8)
        LN_EPS = 1e-05

        def _make_mask(key, n):
            n_proto = n - 1
            adj = jax.random.bernoulli(key, 0.03, (n_proto, n_proto)).astype(jnp.float32)
            adj = jnp.clip(adj + adj.T + jnp.eye(n_proto, dtype=jnp.float32), 0.0, 1.0)
            mask = jnp.zeros((n, n), dtype=jnp.float32)
            mask = mask.at[0, :].set(1.0).at[:, 0].set(1.0)
            mask = mask.at[1:, 1:].set(adj)
            return mask
        key = jax.random.key(seed)
        ks = jax.random.split(key, 7)
        s = 1.0 / np.sqrt(D)
        return {'x': jax.random.normal(ks[0], (B, N, D), dtype=jnp.float32), 'w_qkv': jax.random.uniform(ks[1], (D, 3 * D), dtype=jnp.float32, minval=-s, maxval=s), 'w_proj': jax.random.uniform(ks[2], (D, D), dtype=jnp.float32, minval=-s, maxval=s), 'b_proj': jnp.zeros((D,), dtype=jnp.float32), 'ln_gamma': jnp.ones((D,), dtype=jnp.float32), 'ln_beta': jnp.zeros((D,), dtype=jnp.float32), 'attn_mask': _make_mask(ks[3], N)}
    _L2_gnn_all = _L2_gnn_setup()
    _L2_gnn_in = {k: v for k, v in _L2_gnn_all.items() if k in ('w_qkv', 'w_proj', 'b_proj', 'ln_gamma', 'ln_beta')}
    del _L2_gnn_all

    def _L3_gnn_setup():
        import jax, jax.numpy as jnp
        import numpy as np
        B, N, D, H = (4, 1024, 256, 8)
        HD = D // H
        key = jax.random.key(seed)
        ks = jax.random.split(key, 10)
        x = jax.random.normal(ks[0], (B, N, D), dtype=jnp.float32)
        adj = (jax.random.uniform(ks[1], (N, N)) < 0.1).astype(jnp.float32)
        s = 1.0 / np.sqrt(D)
        Wq = jax.random.normal(ks[2], (D, D), dtype=jnp.float32) * s
        Wk = jax.random.normal(ks[3], (D, D), dtype=jnp.float32) * s
        Wv = jax.random.normal(ks[4], (D, D), dtype=jnp.float32) * s
        Wo = jax.random.normal(ks[5], (D, D), dtype=jnp.float32) * s
        bq = jnp.zeros((D,), jnp.float32)
        bk = jnp.zeros((D,), jnp.float32)
        bv = jnp.zeros((D,), jnp.float32)
        bo = jnp.zeros((D,), jnp.float32)
        return {'x': x, 'adj': adj, 'Wq': Wq, 'bq': bq, 'Wk': Wk, 'bk': bk, 'Wv': Wv, 'bv': bv, 'Wo': Wo, 'bo': bo}
    _L3_gnn_all = _L3_gnn_setup()
    _L3_gnn_in = {k: v for k, v in _L3_gnn_all.items() if k in ('Wq', 'bq', 'Wk', 'bk', 'Wv', 'bv', 'Wo', 'bo')}
    del _L3_gnn_all
    return {'x': x, 'adj': adj, 'L0_gnn_weight': _L0_gnn_in['weight'], 'L0_gnn_bias': _L0_gnn_in['bias'], 'L1_gnn_weight': _L1_gnn_in['weight'], 'L1_gnn_bias': _L1_gnn_in['bias'], 'L2_gnn_w_qkv': _L2_gnn_in['w_qkv'], 'L2_gnn_w_proj': _L2_gnn_in['w_proj'], 'L2_gnn_b_proj': _L2_gnn_in['b_proj'], 'L2_gnn_ln_gamma': _L2_gnn_in['ln_gamma'], 'L2_gnn_ln_beta': _L2_gnn_in['ln_beta'], 'L3_gnn_Wq': _L3_gnn_in['Wq'], 'L3_gnn_bq': _L3_gnn_in['bq'], 'L3_gnn_Wk': _L3_gnn_in['Wk'], 'L3_gnn_bk': _L3_gnn_in['bk'], 'L3_gnn_Wv': _L3_gnn_in['Wv'], 'L3_gnn_bv': _L3_gnn_in['bv'], 'L3_gnn_Wo': _L3_gnn_in['Wo'], 'L3_gnn_bo': _L3_gnn_in['bo']}

def reference(x, adj, L0_gnn_weight, L0_gnn_bias, L1_gnn_weight, L1_gnn_bias, L2_gnn_w_qkv, L2_gnn_w_proj, L2_gnn_b_proj, L2_gnn_ln_gamma, L2_gnn_ln_beta, L3_gnn_Wq, L3_gnn_bq, L3_gnn_Wk, L3_gnn_bk, L3_gnn_Wv, L3_gnn_bv, L3_gnn_Wo, L3_gnn_bo):
    import jax
    import jax.numpy as jnp

    def _L0_gnn_ref(x, adj, weight, bias):
        import jax, jax.numpy as jnp
        import numpy as np
        B, N, D, O = (8, 2048, 256, 256)
        y = jnp.einsum('nm,bmd->bnd', adj, x)
        out = jnp.einsum('bnd,do->bno', y, weight) + bias
        return out

    def _L1_gnn_ref(x, adj, weight, bias):
        import jax, jax.numpy as jnp
        import numpy as np
        B, N, F_IN, F_OUT = (16, 1024, 256, 256)
        deg = adj.sum(axis=1)
        deg_inv_sqrt = jnp.where(deg > 0, jax.lax.rsqrt(deg), 0.0)
        norm_adj = adj * deg_inv_sqrt[:, None] * deg_inv_sqrt[None, :]
        support = jnp.einsum('bni,io->bno', x, weight)
        output = jnp.einsum('nm,bmo->bno', norm_adj, support)
        return output + bias

    def _L2_gnn_ref(x, w_qkv, w_proj, b_proj, ln_gamma, ln_beta, attn_mask):
        import jax, jax.numpy as jnp
        import numpy as np
        B, N, D, H = (16, 1025, 256, 8)
        LN_EPS = 1e-05

        def _make_mask(key, n):
            n_proto = n - 1
            adj = jax.random.bernoulli(key, 0.03, (n_proto, n_proto)).astype(jnp.float32)
            adj = jnp.clip(adj + adj.T + jnp.eye(n_proto, dtype=jnp.float32), 0.0, 1.0)
            mask = jnp.zeros((n, n), dtype=jnp.float32)
            mask = mask.at[0, :].set(1.0).at[:, 0].set(1.0)
            mask = mask.at[1:, 1:].set(adj)
            return mask
        b, n, d = x.shape
        hd = d // H
        scale = hd ** (-0.5)
        qkv = (x @ w_qkv).reshape(b, n, 3, H, hd).transpose(2, 0, 3, 1, 4)
        q, k, v = (qkv[0], qkv[1], qkv[2])
        attn = jnp.einsum('bhnd,bhmd->bhnm', q, k) * scale
        attn = jnp.where(attn_mask[None, None] == 0, -jnp.inf, attn)
        attn = jax.nn.softmax(attn, axis=-1)
        o = jnp.einsum('bhnm,bhmd->bhnd', attn, v).transpose(0, 2, 1, 3).reshape(b, n, d)
        o = o @ w_proj + b_proj
        mu = jnp.mean(o, axis=-1, keepdims=True)
        var = jnp.mean(jnp.square(o - mu), axis=-1, keepdims=True)
        ln = (o - mu) * jax.lax.rsqrt(var + LN_EPS) * ln_gamma + ln_beta
        return o + ln

    def _L3_gnn_ref(x, adj, Wq, bq, Wk, bk, Wv, bv, Wo, bo):
        import jax, jax.numpy as jnp
        import numpy as np
        B, N, D, H = (4, 1024, 256, 8)
        HD = D // H
        b, n, d = x.shape
        q = (x @ Wq + bq).reshape(b, n, H, HD)
        k = (x @ Wk + bk).reshape(b, n, H, HD)
        v = (x @ Wv + bv).reshape(b, n, H, HD)
        scores = jnp.einsum('bqhd,bkhd->bhqk', q, k) / jnp.sqrt(jnp.float32(HD))
        scores = scores + (1.0 - adj)[None, None, :, :] * -1000000000.0
        attn = jax.nn.softmax(scores, axis=-1)
        out = jnp.einsum('bhqk,bkhd->bqhd', attn, v).reshape(b, n, d)
        return out @ Wo + bo
    h = jnp.maximum(_layernorm(x, axis=-1), 0.0)
    x = x + _L0_gnn_ref(h, adj, L0_gnn_weight, L0_gnn_bias)
    h = jnp.maximum(_layernorm(x, axis=-1), 0.0)
    x = x + _L1_gnn_ref(h, adj, L1_gnn_weight, L1_gnn_bias)
    h = jnp.maximum(_layernorm(x, axis=-1), 0.0)
    x = x + _L2_gnn_ref(h, L2_gnn_w_qkv, L2_gnn_w_proj, L2_gnn_b_proj, L2_gnn_ln_gamma, L2_gnn_ln_beta, adj)
    h = jnp.maximum(_layernorm(x, axis=-1), 0.0)
    x = x + _L3_gnn_ref(h, adj, L3_gnn_Wq, L3_gnn_bq, L3_gnn_Wk, L3_gnn_bk, L3_gnn_Wv, L3_gnn_bv, L3_gnn_Wo, L3_gnn_bo)
    return x

_drawn_inputs = setup_inputs


def setup_inputs(seed=0):
    import zlib

    import numpy as np

    out = dict(_drawn_inputs(seed))
    spreads = {'L1_gnn_bias': (0.0, 0.1),
     'L2_gnn_b_proj': (0.0, 0.1),
     'L2_gnn_ln_gamma': (1.0, 0.2),
     'L2_gnn_ln_beta': (0.0, 0.1),
     'L3_gnn_bq': (0.0, 0.1),
     'L3_gnn_bk': (0.0, 0.1),
     'L3_gnn_bv': (0.0, 0.282),
     'L3_gnn_bo': (0.0, 0.267)}
    factors = {'L0_gnn_bias': 8.0}
    for name, (base, spread) in spreads.items():
        noise = np.random.default_rng([zlib.crc32(name.encode()), seed]).standard_normal(out[name].shape)
        drawn = base * np.exp(spread * noise) if base else spread * noise
        out[name] = jnp.asarray(drawn.astype(out[name].dtype))
    for name, factor in factors.items():
        out[name] = (out[name] * factor).astype(out[name].dtype)
    return out
```

```python
from contextlib import ExitStack

import concourse.bass as bass
from concourse import mybir

F32 = mybir.dt.float32
F32R = mybir.dt.float32r
ALU = mybir.AluOpType
ACT = mybir.ActivationFunctionType
AX_X = mybir.AxisListType.X

P = 128
EPS = 1e-5
HEADS = 8
BIG = 3.0e38


def wait_apart(eng, begun, sem, value):
    value = value if isinstance(value, int) else eng.to_reg(value)
    eng.wait_ge(begun, 1)
    eng.wait_ge(sem, value)


def make_identity(nc, pool, ident, made):
    nc.gpsimd.memset(ident[:], 0.0).then_inc(made, 1)
    pool.wait_ge(made, 1)
    nc.gpsimd.affine_select(out=ident[:], in_=ident[:], compare_op=ALU.not_equal, fill=1.0, base=0,
                            pattern=[[-1, P]], channel_multiplier=1).then_inc(made, 1)


def graph_phase(nc, a, x_mid, mask):
    B, N, D = a["x"].shape
    NT, DC = N // P, D // P
    HALF = N // 2
    HT = HALF // P
    PAIRS = B // 2
    YG = 2 * DC
    with ExitStack() as ctx:
        def sb(name, shape, dt=F32):
            return ctx.enter_context(nc.sbuf_tensor("g_" + name, shape, dt))

        def sem(name):
            return ctx.enter_context(nc.semaphore("g_" + name))

        ident = sb("ident", [P, P])
        adjT_hi = sb("adjT_hi", [P, NT, N], F32R)
        adjT_lo = sb("adjT_lo", [P, NT, N], F32R)
        x_sb = [sb(f"x{i}", [P, NT, D]) for i in range(2)]
        hn = sb("hn", [P, NT, D])
        h_hi = [sb(f"h_hi{i}", [P, NT, D], F32R) for i in range(2)]
        h_lo = [sb(f"h_lo{i}", [P, NT, D], F32R) for i in range(2)]
        yT_hi = sb("yT_hi", [P, DC, N], F32R)
        yT_lo = sb("yT_lo", [P, DC, N], F32R)
        w_raw = sb("w_raw", [P, 2, DC, D])
        w_hi = sb("w_hi", [P, 2, DC, D], F32R)
        w_lo = sb("w_lo", [P, 2, DC, D], F32R)
        bias = sb("bias", [P, 2, D])
        stats = sb("stats", [P, NT, 6])
        mv = sb("mv", [P, NT, 2])
        var_eps = sb("var_eps", [P, NT])
        rstd = sb("rstd", [P, NT])
        half_neg = sb("half_neg", [P, NT])
        deg = sb("deg", [P, NT])
        deg_pos = sb("deg_pos", [P, NT])
        deg_floor = sb("deg_floor", [P, NT])
        deg_is = sb("deg_is", [P, NT])
        spare = sb("spare", [P, NT])
        ps = [ctx.enter_context(nc.psum_tensor(f"g_ps{i}", [P, 512], F32)) for i in range(8)]
        y_ps, w_ps = ps[:4], ps[4:]

        made = sem("made")
        adj_in = sem("adj_in")
        w_in = sem("w_in")
        x_in = [sem(f"x_in{i}") for i in range(2)]
        x_stored = [sem(f"x_stored{i}") for i in range(2)]
        at_mm = sem("at_mm")
        at_hi = sem("at_hi")
        at_free = sem("at_free")
        w_hi_done = sem("w_hi_done")
        w_split = sem("w_split")
        deg_done = sem("deg_done")
        r_chain = sem("r_chain")
        stat_done = sem("stat_done")
        mv_done = sem("mv_done")
        ln_chain = sem("ln_chain")
        hn_done = sem("hn_done")
        xb_done = sem("xb_done")
        relu_hi = sem("relu_hi")
        h_done = sem("h_done")
        y_mm = sem("y_mm")
        y_hi_done = sem("y_hi_done")
        y_free = sem("y_free")
        w_mm = sem("w_mm")
        w_free = sem("w_free")
        mask_done = sem("mask_done")
        block = ctx.enter_context(nc.Block())

        AT = 2 * NT

        @block.sync
        def _(sp):
            for t in range(NT):
                sp.dma_start(mask[:, t, :], a["adj"][t * P:(t + 1) * P, :]).then_inc(adj_in, 16)
            for s in range(2):
                sp.dma_start(x_sb[s][:], a["x"][s].rearrange("(t p) d -> p t d", p=P)).then_inc(x_in[s], 16)
            for layer, name in enumerate(("L0_gnn", "L1_gnn")):
                sp.dma_start(w_raw[:, layer], a[name + "_weight"].rearrange("(c p) o -> p c o", p=P)).then_inc(w_in, 16)
                sp.dma_start(bias[:, layer], a[name + "_bias"].partition_broadcast(P)).then_inc(w_in, 16)

            def move(pair, s, more):
                wait_apart(sp, adj_in, w_free, 16 * pair + 4 * (s + 4))
                sp.dma_start(x_mid[2 * pair + s].rearrange("(t p) d -> p t d", p=P), x_sb[s][:]).then_inc(x_stored[s], 16)
                wait_apart(sp, adj_in, x_stored[s], 16 * pair + 16)
                if more:
                    sp.dma_start(x_sb[s][:], a["x"][2 * pair + 2 + s].rearrange("(t p) d -> p t d", p=P)).then_inc(x_in[s], 16)

            with sp.Fori(0, PAIRS - 1) as pair:
                for s in range(2):
                    move(pair, s, True)
            for s in range(2):
                move(PAIRS - 1, s, False)

        @block.tensor
        def _(pe):
            mm = nc.tensor.matmul
            pe.wait_ge(made, 2)
            for n in range(AT):
                m, nh = n % NT, n // NT
                pe.wait_ge(adj_in, 16 * NT)
                if n >= 8:
                    pe.wait_ge(at_free, n - 7)
                for i in range(HT):
                    last = nc.tensor.transpose(ps[n % 8][:, i * P:(i + 1) * P],
                                               mask[:, nh * HT + i, m * P:(m + 1) * P], ident[:])
                last.then_inc(at_mm, 1)

            def split_product(out, stat, mov, first, final):
                (s_hi, s_lo), (m_hi, m_lo) = stat, mov
                mm(out, s_hi, m_hi, start=first, stop=False)
                mm(out, s_hi, m_lo, start=False, stop=False)
                return mm(out, s_lo, m_hi, start=False, stop=final)

            def y_group(job, g, s):
                nh, c = g // DC, g % DC
                pe.wait_ge(y_free, 4 * job + g + 1)
                for m in range(NT):
                    stat = (h_hi[s][:, m, c * P:(c + 1) * P], h_lo[s][:, m, c * P:(c + 1) * P])
                    mov = (adjT_hi[:, m, nh * HALF:(nh + 1) * HALF], adjT_lo[:, m, nh * HALF:(nh + 1) * HALF])
                    last = split_product(y_ps[g][:], stat, mov, m == 0, m == NT - 1)
                last.then_inc(y_mm, 1)

            def w_blocks(job, layer, qs):
                for q in qs:
                    pe.wait_ge(y_free, 4 * job + DC * (q // 2 + 1) + 4)
                    pe.wait_ge(w_free, 4 * job + q + 1)
                    for i in range(2):
                        t = 2 * q + i
                        for c in range(DC):
                            stat = (yT_hi[:, c, t * P:(t + 1) * P], yT_lo[:, c, t * P:(t + 1) * P])
                            mov = (w_hi[:, layer, c, :], w_lo[:, layer, c, :])
                            last = split_product(w_ps[q][:, i * D:(i + 1) * D], stat, mov, c == 0, c == DC - 1)
                    last.then_inc(w_mm, 1)

            def pair_jobs(pair):
                for k in range(4):
                    job = 4 * pair + k
                    pe.wait_ge(h_done, job + 1)
                    y_group(job, 0, k % 2)
                    if k > 0:
                        w_blocks(job - 1, (k - 1) // 2, (2, 3))
                    y_group(job, 1, k % 2)
                    y_group(job, 2, k % 2)
                    w_blocks(job, k // 2, (0, 1))
                    y_group(job, 3, k % 2)
                w_blocks(4 * pair + 3, 1, (2, 3))

            pe.wait_ge(at_free, AT)
            pe.wait_ge(w_split, 1)
            with pe.Fori(0, PAIRS) as pair:
                pair_jobs(pair)

        @block.scalar
        def _(act):
            for n in range(AT):
                m, nh = n % NT, n // NT
                act.wait_ge(at_mm, n + 1)
                nc.scalar.activation(adjT_hi[:, m, nh * HALF:(nh + 1) * HALF], ps[n % 8][:], ACT.Copy).then_inc(at_hi, 1)
            act.wait_ge(w_in, 64)
            nc.scalar.activation(w_hi[:], w_raw[:], ACT.Copy).then_inc(w_hi_done, 1)
            with act.Fori(0, 4 * PAIRS) as job:
                for g in range(YG):
                    nh, c = g // DC, g % DC
                    act.wait_ge(y_mm, 4 * job + g + 1)
                    nc.scalar.activation(yT_hi[:, c, nh * HALF:(nh + 1) * HALF], y_ps[g][:], ACT.Copy).then_inc(y_hi_done, 1)

        @block.gpsimd
        def _(pool):
            make_identity(nc, pool, ident, made)
            nc.gpsimd.memset(half_neg[:], -0.5).then_inc(made, 1)
            pool.wait_ge(made, 3)

            def norm(job, k):
                layer, s = k // 2, k % 2
                wait_apart(pool, made, mv_done, job + 1)
                nc.gpsimd.tensor_scalar(var_eps[:], mv[:, :, 1], EPS, None, ALU.add).then_inc(ln_chain, 1)
                pool.wait_ge(ln_chain, 3 * job + 1)
                nc.gpsimd.tensor_tensor(rstd[:], var_eps[:], half_neg[:], op=ALU.pow).then_inc(ln_chain, 1)
                wait_apart(pool, made, ln_chain, 3 * job + 2)
                scale = deg_is if layer else None
                if layer:
                    nc.gpsimd.tensor_tensor(rstd[:], rstd[:], scale[:], op=ALU.mult).then_inc(ln_chain, 1)
                else:
                    nc.gpsimd.tensor_copy(var_eps[:], rstd[:]).then_inc(ln_chain, 1)
                wait_apart(pool, made, ln_chain, 3 * job + 3)
                for t in range(NT):
                    nc.gpsimd.tensor_scalar(hn[:, t, :], x_sb[s][:, t, :], mv[:, t, 0:1], rstd[:, t:t + 1],
                                            ALU.subtract, ALU.mult).then_inc(hn_done, 1)
                pool.wait_ge(hn_done, 8 * job + 8)
                nc.gpsimd.tensor_tensor(x_sb[s][:], x_sb[s][:],
                                        bias[:, layer:layer + 1, :].to_broadcast([P, NT, D]), op=ALU.add).then_inc(xb_done, 1)

            pool.wait_ge(w_in, 64)
            norm(0, 0)
            pool.wait_ge(deg_done, NT)
            nc.gpsimd.tensor_scalar(deg_floor[:], deg[:], 1e-30, None, ALU.max).then_inc(r_chain, 1)
            nc.gpsimd.tensor_scalar(deg_pos[:], deg[:], 0.0, None, ALU.is_gt).then_inc(r_chain, 1)
            pool.wait_ge(r_chain, 2)
            nc.gpsimd.tensor_tensor(deg_is[:], deg_floor[:], half_neg[:], op=ALU.pow).then_inc(r_chain, 1)
            pool.wait_ge(r_chain, 3)
            nc.gpsimd.tensor_tensor(deg_is[:], deg_is[:], deg_pos[:], op=ALU.mult).then_inc(r_chain, 1)
            pool.wait_ge(r_chain, 4)
            with pool.Fori(0, PAIRS - 1) as pair:
                for k in range(4):
                    norm(4 * pair + k + 1, (k + 1) % 4)
            for k in range(3):
                norm(4 * (PAIRS - 1) + k + 1, k + 1)

        @block.vector
        def _(dve):
            def ln_stats(job, k):
                s = k % 2
                if not (isinstance(job, int) and job == 0):
                    dve.wait_ge(w_free, 4 * job)
                for t in range(NT):
                    nc.vector.bn_stats(stats[:, t, :], x_sb[s][:, t, :]).then_inc(stat_done, 1)
                wait_apart(dve, made, stat_done, 8 * job + 8)
                for t in range(NT):
                    last = nc.vector.bn_aggr(mv[:, t, :], stats[:, t, :])
                last.then_inc(mv_done, 1)

            def relu_split(job, k):
                s = k % 2
                for th in range(2):
                    part = slice(th * HT, (th + 1) * HT)
                    dve.wait_ge(hn_done, 8 * job + 4 * th + 4)
                    nc.vector.tensor_scalar(h_hi[s][:, part, :], hn[:, part, :], 0.0, None, ALU.max).then_inc(relu_hi, 1)
                    dve.wait_ge(relu_hi, 2 * job + th + 1)
                    last = nc.vector.scalar_tensor_tensor(
                        out=h_lo[s][:, part, :], in0=hn[:, part, :], scalar=0.0,
                        in1=h_hi[s][:, part, :].bitcast(F32), op0=ALU.max, op1=ALU.subtract)
                last.then_inc(h_done, 1)

            def y_lo(job, g):
                nh, c = g // DC, g % DC
                dve.wait_ge(y_hi_done, 4 * job + g + 1)
                cols = slice(nh * HALF, (nh + 1) * HALF)
                nc.vector.tensor_tensor(yT_lo[:, c, cols], y_ps[g][:], yT_hi[:, c, cols].bitcast(F32),
                                        op=ALU.subtract).then_inc(y_free, 1)

            def add_out(job, k, qs):
                layer, s = k // 2, k % 2
                dve.wait_ge(xb_done, job + 1)
                for q in qs:
                    dve.wait_ge(w_mm, 4 * job + q + 1)
                    for i in range(2):
                        t = 2 * q + i
                        last = nc.vector.scalar_tensor_tensor(
                            out=x_sb[s][:, t, :], in0=w_ps[q][:, i * D:(i + 1) * D],
                            scalar=deg_is[:, t:t + 1] if layer else 1.0, in1=x_sb[s][:, t, :],
                            op0=ALU.mult, op1=ALU.add)
                    last.then_inc(w_free, 1)

            dve.wait_ge(x_in[0], 16)
            ln_stats(0, 0)
            for n in range(AT):
                m, nh = n % NT, n // NT
                if n % 2 == 0:
                    dve.wait_ge(adj_in, 16 * NT)
                    nc.vector.reduce_sum(deg[:, n // 2:n // 2 + 1], mask[:, n // 2, :], axis=AX_X).then_inc(deg_done, 1)
                dve.wait_ge(at_hi, n + 1)
                cols = slice(nh * HALF, (nh + 1) * HALF)
                nc.vector.tensor_tensor(adjT_lo[:, m, cols], ps[n % 8][:], adjT_hi[:, m, cols].bitcast(F32),
                                        op=ALU.subtract).then_inc(at_free, 1)
            dve.wait_ge(w_hi_done, 1)
            nc.vector.tensor_tensor(w_lo[:], w_raw[:], w_hi[:].bitcast(F32), op=ALU.subtract).then_inc(w_split, 1)
            relu_split(0, 0)
            for t in range(NT):
                nc.vector.memset(spare[:, t:t + 1], 0.0).then_inc(y_free if t < 4 else w_free, 1)

            def slot(pair, k, more, carry):
                job = 4 * pair + k
                if carry:
                    add_out(job - 1, k - 1, (2, 3))
                y_lo(job, 0)
                if k == 3:
                    y_lo(job, 1)
                if more:
                    if k == 3:
                        dve.wait_ge(x_in[0], 16 * pair + 32)
                    if k == 0:
                        dve.wait_ge(x_in[1], 16 * pair + 16)
                    ln_stats(job + 1, (k + 1) % 4)
                if k != 3:
                    y_lo(job, 1)
                y_lo(job, 2)
                if more:
                    relu_split(job + 1, (k + 1) % 4)
                add_out(job, k, (0, 1))
                y_lo(job, 3)

            with dve.Fori(0, PAIRS - 1) as pair:
                for k in range(4):
                    slot(pair, k, True, k > 0)
                add_out(4 * pair + 3, 3, (2, 3))
            for k in range(4):
                slot(PAIRS - 1, k, k < 3, k > 0)
            add_out(4 * PAIRS - 1, 3, (2, 3))
            dve.wait_ge(at_mm, AT)
            for t in range(NT):
                nc.vector.tensor_scalar(mask[:, t, :], mask[:, t, :], 0.0, BIG, ALU.is_equal, ALU.mult).then_inc(mask_done, 1)
            dve.wait_ge(mask_done, NT)


UNITS = 64
EARLY = [(5, ("norm", 3)), (6, ("turn", 0)), (8, ("out", 0)), (9, ("turn", 1)), (11, ("out", 1)),
         (12, ("turn", 2)), (14, ("out", 2)), (15, ("turn", 3)), (17, ("out", 3))]
MID = [(18, ("qk", 1, 0, 0)), (20, ("qk", 1, 1, 0)), (21, ("norm", 0)), (22, ("qk", 1, 0, 1)),
       (23, ("qk", 1, 1, 1)), (24, ("v", 1, 0)), (26, ("v", 1, 1)), (37, ("norm", 1)), (53, ("norm", 2))]
NEXT = [(38, ("h", 0, 0)), (40, ("h", 0, 1)), (42, ("h", 1, 0)), (44, ("h", 1, 1)),
        (46, ("v", 0, 0)), (47, ("v", 0, 1)),
        (48, ("qk", 0, 0, 0)), (50, ("qk", 0, 1, 0)), (52, ("qk", 0, 0, 1)), (54, ("qk", 0, 1, 1))]
PER_JOB = len(EARLY) + len(MID) + len(NEXT)


def blocks_of(first, core, more):
    table = sorted((EARLY if not first else []) + (MID if core else []) + (NEXT if more else []))
    skip = len(EARLY) if first else 0
    return {step: (skip + i, what) for i, (step, what) in enumerate(table)}


def attention_phase(nc, a, x_mid, x_mid2, out, mask):
    B, N, D = a["x"].shape
    NT, DC = N // P, D // P
    HD = D // HEADS
    HALF = N // 2
    HT = HALF // P
    JOBS = 2 * B
    SCALE = float(HD) ** -0.5
    GH = P // HD
    RING = 4
    with ExitStack() as ctx:
        def sb(name, shape, dt=F32):
            return ctx.enter_context(nc.sbuf_tensor("t_" + name, shape, dt))

        def sem(name):
            return ctx.enter_context(nc.semaphore("t_" + name))

        def pb(name, width):
            return ctx.enter_context(nc.psum_tensor("t_" + name, [P, width], F32))

        ident = sb("ident", [P, P])
        w_hi = [sb(f"w_hi{i}", [P, DC, 4 * D], F32R) for i in range(2)]
        w_lo = [sb(f"w_lo{i}", [P, DC, 4 * D], F32R) for i in range(2)]
        b_qk = sb("b_qk", [P, 2, 2, 2])
        b_v = [sb(f"b_v{i}", [P, 1, D]) for i in range(2)]
        b_out = [sb(f"b_out{i}", [P, 1, D]) for i in range(2)]
        gamma = sb("gamma", [P, 1, D])
        beta = sb("beta", [P, 1, D])
        xa = sb("xa", [P, NT, D])
        hT_hi = sb("hT_hi", [P, DC, N], F32R)
        hT_lo = sb("hT_lo", [P, DC, N], F32R)
        st_hi = [sb(f"st_hi{i}", [P, N], F32R) for i in range(2)]
        st_lo = [sb(f"st_lo{i}", [P, N], F32R) for i in range(2)]
        q4 = [sb(f"q4_{i}", [P, N], F32R) for i in range(2)]
        k4 = [sb(f"k4_{i}", [P, N], F32R) for i in range(2)]
        v_sb = sb("v", [P, NT, D])
        T = [sb(f"T{i}", [P, N]) for i in range(RING)]
        PT = [sb(f"PT{i}", [P, 4, NT, P]) for i in range(2)]
        low = sb("low", [P, RING])
        rsum = sb("rsum", [P, UNITS])
        rinv = sb("rinv", [P, UNITS])
        ot_sb = sb("ot", [P, 512])
        o_sb = sb("o", [P, NT, D])
        oT_hi = sb("oT_hi", [P, 512], F32R)
        oT_lo = sb("oT_lo", [P, 512], F32R)
        xe = [sb(f"xe{i}", [P, 2, D]) for i in range(2)]
        proj = sb("proj", [P, 2, D])
        ln = sb("ln", [P, 2, D])
        stats = sb("stats", [P, NT, 6])
        mv = sb("mv", [P, NT, 2])
        var_eps = sb("var_eps", [P, NT])
        rstd = sb("rstd", [P, NT])
        half_neg = sb("half_neg", [P, NT])
        stats2 = sb("stats2", [P, 2, 6])
        mv2 = sb("mv2", [P, 2, 2])
        var2 = sb("var2", [P, 2])
        rstd2 = sb("rstd2", [P, 2])

        s_ps = [pb(f"s_ps{i}", N) for i in range(2)]
        pt_ps = [pb(f"pt_ps{i}", 512) for i in range(2)]
        ot_ps = pb("ot_ps", 512)
        g_ps = pb("g_ps", 512)

        made = sem("made")
        raw_in = sem("raw_in")
        bias_in = sem("bias_in")
        bias_done = sem("bias_done")
        w_hi_done = sem("w_hi_done")
        w_split = sem("w_split")
        xa_in = sem("xa_in")
        stat_done = sem("stat_done")
        mv_done = sem("mv_done")
        ln_chain = sem("ln_chain")
        hn_done = sem("hn_done")
        g_mm = sem("g_mm")
        g_free = sem("g_free")
        h_hi_done = sem("h_hi_done")
        qk_hi_done = sem("qk_hi_done")
        oT_hi_done = sem("oT_hi_done")
        head_in = [sem(f"head_in{i}") for i in range(2)]
        s_done = sem("s_done")
        t_done = sem("t_done")
        p_done = sem("p_done")
        tr_done = [sem(f"tr_done{i}") for i in range(2)]
        pt_done = [sem(f"pt_done{i}") for i in range(2)]
        av_done = sem("av_done")
        ot_done = sem("ot_done")
        rinv_done = sem("rinv_done")
        xe_in = [sem(f"xe_in{i}") for i in range(2)]
        xe_biased = sem("xe_biased")
        x_stored = sem("x_stored")
        stat2_done = sem("stat2_done")
        mv2_done = sem("mv2_done")
        epi_chain = sem("epi_chain")
        epi_done = sem("epi_done")
        mask_in = [sem(f"mask_in{t}") for t in range(NT)]
        mask3_done = sem("mask3_done")
        block = ctx.enter_context(nc.Block())

        FIRST_BLOCKS = len(NEXT)

        def block_at(job, k):
            return PER_JOB * job + FIRST_BLOCKS - len(EARLY) + k

        def jobs(eng, body):
            body(0, 0, None, 0)
            with eng.Fori(1, B - 1) as job:
                body(job, 0, 0, 0)
            body(B - 1, 0, 0, 1)
            body(B, 1, 0, 1)
            with eng.Fori(B + 1, JOBS - 1) as job:
                body(job, 1, 1, 1)
            body(JOBS - 1, 1, 1, None)

        def tail_block(k):
            return block_at(JOBS, k) - len(NEXT)

        def x_of(layer, batch):
            return (x_mid, x_mid2)[layer][batch]

        @block.sync
        def _(sp):
            sp.dma_start(xa[:], x_of(0, 0).rearrange("(t p) d -> p t d", p=P)).then_inc(xa_in, 16)
            raw = [PT[i][:].rearrange("p a b c -> p (a b c)")[:, 0:2 * 4 * D].rearrange("p (c o) -> p c o", c=DC)
                   for i in range(2)]
            sp.dma_start(raw[0][:, :, 0:3 * D], a["L2_gnn_w_qkv"].rearrange("(c p) o -> p c o", p=P)).then_inc(raw_in, 16)
            sp.dma_start(raw[0][:, :, 3 * D:], a["L2_gnn_w_proj"].rearrange("(c p) o -> p c o", p=P)).then_inc(raw_in, 16)
            for i, name in enumerate(("Wq", "Wk", "Wv", "Wo")):
                sp.dma_start(raw[1][:, :, i * D:(i + 1) * D],
                             a["L3_gnn_" + name].rearrange("(c p) o -> p c o", p=P)).then_inc(raw_in, 16)
            for dst, name in ((b_v[1], "L3_gnn_bv"), (b_out[0], "L2_gnn_b_proj"), (b_out[1], "L3_gnn_bo"),
                              (gamma, "L2_gnn_ln_gamma"), (beta, "L2_gnn_ln_beta")):
                sp.dma_start(dst[:, 0, :], a[name].partition_broadcast(P)).then_inc(bias_in, 16)
            for w, name in enumerate(("L3_gnn_bq", "L3_gnn_bk")):
                for g in range(2):
                    sp.dma_start(b_qk[:, 1, w, g:g + 1], a[name][g * P:(g + 1) * P].rearrange("(p o) -> p o", o=1)).then_inc(bias_in, 16)

            def load_head(job, h, slot_free, staged):
                s, rows = h % 2, slice((h % GH) * HD, (h % GH + 1) * HD)
                if slot_free is not None:
                    wait_apart(sp, raw_in, s_done, slot_free)
                if staged is not None:
                    sp.wait_ge(g_free, staged)
                for part in range(4):
                    dst = slice(part * HD, (part + 1) * HD)
                    sp.dma_start(q4[s][dst, :].bitcast(F32), (st_hi, st_lo)[part // 2][0][rows, :].bitcast(F32)).then_inc(head_in[s], 16)
                    sp.dma_start(k4[s][dst, :].bitcast(F32), (st_hi, st_lo)[part % 2][1][rows, :].bitcast(F32)).then_inc(head_in[s], 16)

            def load_xe(job, layer, p):
                batch = job - B * layer
                sp.dma_start(xe[p % 2][:], x_of(layer, batch)[2 * p * P:2 * (p + 1) * P, :]
                             .rearrange("(t p) d -> p t d", p=P)).then_inc(xe_in[p % 2], 16)

            def store(job, layer, p, n):
                batch = job - B * layer
                if layer == 0:
                    wait_apart(sp, raw_in, epi_done, 4 * job + p + 2)
                else:
                    wait_apart(sp, raw_in, g_free, n + 1)
                sp.dma_start((x_mid2, out)[layer][batch, 2 * p * P:2 * (p + 1) * P, :]
                             .rearrange("(t p) d -> p t d", p=P), xe[p % 2][:]).then_inc(x_stored, 16)

            def after_store(job, p):
                wait_apart(sp, raw_in, x_stored, 16 * (4 * job + p + 1))

            def body(job, layer, before, after):
                table = blocks_of(before is None, True, after is not None)
                at = {what: block_at(job, k) for k, what in table.values()}
                if after is not None:
                    wait_apart(sp, raw_in, s_done, UNITS * job + 1)
                    sp.dma_start(xa[:], x_of(after, job + 1 - B * after).rearrange("(t p) d -> p t d", p=P)).then_inc(xa_in, 16)
                if before is not None:
                    load_xe(job - 1, before, 0)
                    load_xe(job - 1, before, 1)
                load_head(job, 2, UNITS * job + 8, None)
                if before is not None:
                    store(job - 1, before, 0, at[("out", 0)])
                    after_store(job - 1, 0)
                    load_xe(job - 1, before, 2)
                    store(job - 1, before, 1, at[("out", 1)])
                    after_store(job - 1, 1)
                    load_xe(job - 1, before, 3)
                load_head(job, 3, UNITS * job + 16, None)
                if before is not None:
                    store(job - 1, before, 2, at[("out", 2)])
                    store(job - 1, before, 3, at[("out", 3)])
                for h in range(4, HEADS):
                    load_head(job, h, UNITS * job + 8 * (h - 1), at[("qk", 1, 1, 1)] + 1 if h == 4 else None)
                if before is not None:
                    after_store(job - 1, 3)
                if after is not None:
                    load_head(job + 1, 0, UNITS * job + 56, at[("qk", 0, 1, 1)] + 1)
                    load_head(job + 1, 1, UNITS * job + 64, None)

            load_head(0, 0, None, FIRST_BLOCKS)
            load_head(0, 1, None, None)
            jobs(sp, body)
            table = blocks_of(False, False, False)
            at = {what: tail_block(k) for k, what in table.values()}
            load_xe(JOBS - 1, 1, 0)
            load_xe(JOBS - 1, 1, 1)
            for p in range(4):
                store(JOBS - 1, 1, p, at[("out", p)])
                if p < 2:
                    after_store(JOBS - 1, p)
                    load_xe(JOBS - 1, 1, p + 2)
            after_store(JOBS - 1, 3)

        @block.tensor
        def _(pe):
            mm = nc.tensor.matmul

            def split_product(dst, stat, mov, first, final):
                (s_hi, s_lo), (m_hi, m_lo) = stat, mov
                mm(dst, s_hi, m_hi, start=first, stop=False)
                mm(dst, s_hi, m_lo, start=False, stop=False)
                return mm(dst, s_lo, m_hi, start=False, stop=final)

            def scores(job, u, wait):
                job, u = (job + 1, u - UNITS) if u >= UNITS else (job, u)
                h, qt = u // NT, u % NT
                if qt == 0:
                    pe.wait_ge(head_in[h % 2], 128 * (4 * job + h // 2 + 1))
                if wait is not None:
                    pe.wait_ge(t_done, wait)
                for half in range(2):
                    cols = slice(half * HALF, (half + 1) * HALF)
                    last = mm(s_ps[u % 2][:, cols], q4[h % 2][:, qt * P:(qt + 1) * P], k4[h % 2][:, cols],
                              start=True, stop=True)
                last.then_inc(s_done, 1)

            def transposes(job, u):
                pe.wait_ge(p_done, UNITS * job + u + 1)
                for half in range(2):
                    pe.wait_ge(pt_done[half], UNITS * job + u + 1)
                    for i in range(HT):
                        kt = half * HT + i
                        last = nc.tensor.transpose(pt_ps[half][:, i * P:(i + 1) * P],
                                                   T[u % RING][:, kt * P:(kt + 1) * P], ident[:])
                    last.then_inc(tr_done[half], 1)

            def values(job, u):
                gr = u // 4 - 1 if u >= 4 else UNITS // 4 - 1
                h, col = gr // 2, gr % 4
                if u % 4 == 0:
                    pe.wait_ge(pt_done[0], UNITS * job + u + 1)
                    pe.wait_ge(pt_done[1], UNITS * job + u + 1)
                    if col == 0:
                        pair_no = 4 * job + gr // 4 if u >= 4 else 4 * job - 1
                        if not (isinstance(job, int) and pair_no == 0):
                            pe.wait_ge(ot_done, pair_no)
                for kt in range(2 * (u % 4), 2 * (u % 4) + 2):
                    for j in range(4):
                        last = mm(ot_ps[j * HD:(j + 1) * HD, col * P:(col + 1) * P],
                                  v_sb[:, kt, h * HD:(h + 1) * HD], PT[gr % 2][:, j, kt, :],
                                  start=kt == 0, stop=kt == NT - 1)
                last.then_inc(av_done, 1)

            def one_block(n, what, layer, job_of_h):
                if not (isinstance(n, int) and n == 0):
                    pe.wait_ge(g_free, n)
                kind = what[0]
                if kind == "norm":
                    for i in range(4):
                        last = nc.tensor.transpose(g_ps[:, i * P:(i + 1) * P], ot_sb[:, i * P:(i + 1) * P], ident[:])
                elif kind == "turn":
                    for i in range(4):
                        t, c = 2 * what[1] + i // DC, i % DC
                        last = nc.tensor.transpose(g_ps[:, i * P:(i + 1) * P], o_sb[:, t, c * P:(c + 1) * P], ident[:])
                elif kind == "out":
                    for i in range(2):
                        for c in range(DC):
                            at = slice((DC * i + c) * P, (DC * i + c + 1) * P)
                            cols = slice(3 * D, 4 * D)
                            last = split_product(g_ps[:, i * D:(i + 1) * D], (oT_hi[:, at], oT_lo[:, at]),
                                                 (w_hi[layer][:, c, cols], w_lo[layer][:, c, cols]), c == 0, c == DC - 1)
                elif kind == "h":
                    c, nh = what[1:]
                    pe.wait_ge(hn_done, 8 * job_of_h + 4 * nh + 4)
                    for i in range(HT):
                        last = nc.tensor.transpose(g_ps[:, i * P:(i + 1) * P],
                                                   xa[:, nh * HT + i, c * P:(c + 1) * P], ident[:])
                elif kind == "qk":
                    g, w, nh = what[1:]
                    cols, toks = slice(w * D + g * P, w * D + (g + 1) * P), slice(nh * HALF, (nh + 1) * HALF)
                    for c in range(DC):
                        last = split_product(g_ps[:], (w_hi[layer][:, c, cols], w_lo[layer][:, c, cols]),
                                             (hT_hi[:, c, toks], hT_lo[:, c, toks]), c == 0, c == DC - 1)
                else:
                    g, nh = what[1:]
                    cols = slice(2 * D + g * P, 2 * D + (g + 1) * P)
                    for i in range(HT):
                        toks = slice((nh * HT + i) * P, (nh * HT + i + 1) * P)
                        for c in range(DC):
                            last = split_product(g_ps[:, i * P:(i + 1) * P], (hT_hi[:, c, toks], hT_lo[:, c, toks]),
                                                 (w_hi[layer][:, c, cols], w_lo[layer][:, c, cols]), c == 0, c == DC - 1)
                last.then_inc(g_mm, 1)

            def body(job, layer, before, after):
                table = blocks_of(before is None, True, after is not None)
                for u in range(UNITS):
                    if u + 2 < UNITS or after is not None:
                        scores(job, u + 2, UNITS * job + u + 1)
                    if u in table:
                        k, what = table[u]
                        lay = before if (u, what) in EARLY else after if (u, what) in NEXT else layer
                        if what[0] == "norm" and True:
                            pe.wait_ge(ot_done, 4 * job + what[1] + 1 if what[1] < 3 else 4 * job)
                        one_block(block_at(job, k), what, lay, job + 1)
                    transposes(job, u)
                    if u >= 4 or before is not None:
                        values(job, u)

            pe.wait_ge(made, 3)
            pe.wait_ge(w_split, 2)
            for n, (_, what) in enumerate(NEXT):
                one_block(n, what, 0, 0)
            scores(0, 0, None)
            scores(0, 1, None)
            jobs(pe, body)
            for u in range(4):
                values(JOBS, u)
            for k, what in blocks_of(False, False, False).values():
                if what[0] == "norm":
                    pe.wait_ge(ot_done, 4 * JOBS)
                one_block(tail_block(k), what, 1, None)

        @block.scalar
        def _(act):
            copy = nc.scalar.activation

            def hi_part(n, what, layer, job):
                kind = what[0]
                if kind == "h":
                    c, nh = what[1:]
                    act.wait_ge(g_mm, n + 1)
                    copy(hT_hi[:, c, nh * HALF:(nh + 1) * HALF], g_ps[:], ACT.Relu).then_inc(h_hi_done, 1)
                elif kind == "qk":
                    g, w, nh = what[1:]
                    if not (g == 0 and isinstance(job, int) and job == 0):
                        for s in range(2):
                            act.wait_ge(head_in[s], 128 * (4 * job + 2 * g))
                    act.wait_ge(g_mm, n + 1)
                    copy(st_hi[w][:, nh * HALF:(nh + 1) * HALF], g_ps[:], ACT.Identity,
                         bias=b_qk[:, layer, w, g:g + 1]).then_inc(qk_hi_done, 1)
                elif kind == "turn":
                    act.wait_ge(g_mm, n + 1)
                    copy(oT_hi[:], g_ps[:], ACT.Copy).then_inc(oT_hi_done, 1)

            def exp(job, u):
                job, u = (job + 1, u - UNITS) if u >= UNITS else (job, u)
                act.wait_ge(t_done, UNITS * job + u + 1)
                nc.scalar.activation(T[u % RING][:], T[u % RING][:], ACT.Exp, bias=low[:, u % RING:u % RING + 1],
                                     scale=-1.0, accum_out=rsum[:, u:u + 1]).then_inc(p_done, 1)

            def copy_pt(job, u, half):
                act.wait_ge(tr_done[half], UNITS * job + u + 1)
                copy(PT[u // 4 % 2][:, u % 4, half * HT:(half + 1) * HT, :],
                     pt_ps[half][:].rearrange("p (k q) -> p k q", k=HT), ACT.Copy).then_inc(pt_done[half], 1)

            def copy_ot(after):
                act.wait_ge(av_done, after)
                copy(ot_sb[:], ot_ps[:], ACT.Copy).then_inc(ot_done, 1)

            act.wait_ge(raw_in, 96)
            for layer in range(2):
                raw = PT[layer][:].rearrange("p a b c -> p (a b c)")[:, 0:2 * 4 * D].rearrange("p (c o) -> p c o", c=DC)
                copy(w_hi[layer][:, :, 0:D], raw[:, :, 0:D], ACT.Copy, scale=-SCALE).then_inc(w_hi_done, 1)
                copy(w_hi[layer][:, :, D:], raw[:, :, D:], ACT.Copy).then_inc(w_hi_done, 1)
            act.wait_ge(bias_done, 3)
            for n, (_, what) in enumerate(NEXT):
                hi_part(n, what, 0, 0)
            exp(0, 0)

            def body(job, layer, before, after):
                table = blocks_of(before is None, True, after is not None)
                for u in range(UNITS):
                    if u % 16 == 4 and (u >= 20 or before is not None):
                        copy_ot(UNITS * job + u - 4)
                    if u + 1 < UNITS or after is not None:
                        exp(job, u + 1)
                    if u in table:
                        k, what = table[u]
                        in_next = (u, what) in NEXT
                        hi_part(block_at(job, k), what, after if in_next else layer, job + 1 if in_next else job)
                    copy_pt(job, u, 0)
                    if u % 4 == 3:
                        copy_pt(job, u, 1)

            jobs(act, body)
            copy_ot(UNITS * JOBS)
            for k, what in blocks_of(False, False, False).values():
                hi_part(tail_block(k), what, 1, None)

        @block.vector
        def _(dve):
            def masked(job, u, layer):
                job, u = (job + 1, u - UNITS) if u >= UNITS else (job, u)
                qt = u % NT
                if layer == 1 and isinstance(job, int) and job == B:
                    dve.wait_ge(mask3_done, qt + 1)
                wait_apart(dve, made, s_done, UNITS * job + u + 1)
                nc.vector.tensor_tensor_reduce(out=T[u % RING][:], in0=s_ps[u % 2][:], in1=mask[:, qt, :],
                                               scale=1.0, scalar=3.4e38, op0=ALU.add, op1=ALU.min,
                                               accum_out=low[:, u % RING:u % RING + 1]).then_inc(t_done, 1)

            def finish_block(n, what, layer, job):
                kind = what[0]
                if kind == "h":
                    c, nh = what[1:]
                    cols = slice(nh * HALF, (nh + 1) * HALF)
                    dve.wait_ge(h_hi_done, 4 * job + 2 * c + nh + 1)
                    nc.vector.scalar_tensor_tensor(out=hT_lo[:, c, cols], in0=g_ps[:], scalar=0.0,
                                                   in1=hT_hi[:, c, cols].bitcast(F32),
                                                   op0=ALU.max, op1=ALU.subtract).then_inc(g_free, 1)
                elif kind == "qk":
                    g, w, nh = what[1:]
                    cols = slice(nh * HALF, (nh + 1) * HALF)
                    dve.wait_ge(qk_hi_done, 8 * job + 4 * g + 2 * nh + w + 1)
                    nc.vector.scalar_tensor_tensor(out=st_lo[w][:, cols], in0=g_ps[:], scalar=b_qk[:, layer, w, g:g + 1],
                                                   in1=st_hi[w][:, cols].bitcast(F32),
                                                   op0=ALU.add, op1=ALU.subtract).then_inc(g_free, 1)
                elif kind == "v":
                    g, nh = what[1:]
                    dve.wait_ge(g_mm, n + 1)
                    nc.vector.tensor_tensor(v_sb[:, nh * HT:(nh + 1) * HT, g * P:(g + 1) * P],
                                            g_ps[:].rearrange("p (t d) -> p t d", t=HT),
                                            b_v[layer][:, :, g * P:(g + 1) * P].to_broadcast([P, HT, P]),
                                            op=ALU.add).then_inc(g_free, 1)
                elif kind == "norm":
                    pr = what[1]
                    cols = slice(16 * pr, 16 * pr + 16)
                    dve.wait_ge(g_mm, n + 1)
                    nc.vector.reciprocal(rinv[:, cols], rsum[:, cols]).then_inc(rinv_done, 1)
                    dve.wait_ge(rinv_done, 4 * job + pr + 1)
                    nc.vector.tensor_tensor(
                        o_sb[:, :, 2 * pr * HD:(2 * pr + 2) * HD].rearrange("p t (h d) -> p h t d", h=2),
                        g_ps[:].rearrange("p (h t d) -> p h t d", h=2, t=NT),
                        rinv[:, cols].rearrange("p (h t o) -> p h t o", h=2, o=1).to_broadcast([P, 2, NT, HD]),
                        op=ALU.mult).then_inc(g_free, 1)
                elif kind == "turn":
                    dve.wait_ge(oT_hi_done, 4 * job + what[1] + 1)
                    nc.vector.tensor_tensor(oT_lo[:], g_ps[:], oT_hi[:].bitcast(F32), op=ALU.subtract).then_inc(g_free, 1)
                elif layer == 0:
                    p = what[1]
                    dve.wait_ge(epi_done, 4 * job + p + 1)
                    dve.wait_ge(g_mm, n + 1)
                    nc.vector.tensor_tensor(proj[:], g_ps[:].rearrange("p (t d) -> p t d", t=2),
                                            b_out[0][:].to_broadcast([P, 2, D]), op=ALU.add).then_inc(g_free, 1)
                    dve.wait_ge(g_free, n + 1)
                    for i in range(2):
                        nc.vector.bn_stats(stats2[:, i, :], proj[:, i, :]).then_inc(stat2_done, 1)
                    wait_apart(dve, made, stat2_done, 8 * job + 2 * p + 2)
                    for i in range(2):
                        last = nc.vector.bn_aggr(mv2[:, i, :], stats2[:, i, :])
                    last.then_inc(mv2_done, 1)
                else:
                    p = what[1]
                    dve.wait_ge(xe_biased, 4 * job + p + 1)
                    dve.wait_ge(g_mm, n + 1)
                    nc.vector.tensor_tensor(xe[p % 2][:], g_ps[:].rearrange("p (t d) -> p t d", t=2),
                                            xe[p % 2][:], op=ALU.add).then_inc(g_free, 1)

            def copy_pt(job, u):
                dve.wait_ge(tr_done[1], UNITS * job + u + 1)
                nc.vector.tensor_copy(PT[u // 4 % 2][:, u % 4, HT:, :],
                                      pt_ps[1][:].rearrange("p (k q) -> p k q", k=HT)).then_inc(pt_done[1], 1)

            def ln_stats(job, t):
                if t == 0:
                    dve.wait_ge(xa_in, 16 * job + 16)
                nc.vector.bn_stats(stats[:, t, :], xa[:, t, :]).then_inc(stat_done, 1)

            def ln_mean(job):
                wait_apart(dve, made, stat_done, 8 * job + 8)
                for t in range(NT):
                    last = nc.vector.bn_aggr(mv[:, t, :], stats[:, t, :])
                last.then_inc(mv_done, 1)

            for t in range(NT):
                ln_stats(0, t)
            ln_mean(0)
            for layer in range(2):
                raw = PT[layer][:].rearrange("p a b c -> p (a b c)")[:, 0:2 * 4 * D].rearrange("p (c o) -> p c o", c=DC)
                dve.wait_ge(w_hi_done, 2 * layer + 2)
                nc.vector.scalar_tensor_tensor(out=w_lo[layer][:, :, 0:D], in0=raw[:, :, 0:D], scalar=-SCALE,
                                               in1=w_hi[layer][:, :, 0:D].bitcast(F32), op0=ALU.mult, op1=ALU.subtract)
                nc.vector.tensor_tensor(w_lo[layer][:, :, D:], raw[:, :, D:], w_hi[layer][:, :, D:].bitcast(F32),
                                        op=ALU.subtract).then_inc(w_split, 1)
            dve.wait_ge(bias_done, 3)
            for n, (_, what) in enumerate(NEXT):
                finish_block(n, what, 0, 0)
            for half in range(2):
                nc.vector.memset(rinv[:, half:half + 1], 1.0).then_inc(pt_done[half], 1)
            masked(0, 0, 0)
            masked(0, 1, 0)

            def body(job, layer, before, after):
                table = blocks_of(before is None, True, after is not None)
                for u in range(UNITS):
                    if u + 2 < UNITS or after is not None:
                        masked(job, u + 2, layer if u + 2 < UNITS else after)
                    if u in table:
                        k, what = table[u]
                        early, in_next = (u, what) in EARLY, (u, what) in NEXT
                        finish_block(block_at(job, k), what, before if early else after if in_next else layer,
                                     job - 1 if early else job + 1 if in_next else job)
                    if u % 4 != 3:
                        copy_pt(job, u)
                    if after is not None and 27 <= u < 27 + NT:
                        ln_stats(job + 1, u - 27)
                    if after is not None and u == 27 + NT:
                        ln_mean(job + 1)

            jobs(dve, body)
            for k, what in blocks_of(False, False, False).values():
                finish_block(tail_block(k), what, 1, JOBS - 1)

        @block.gpsimd
        def _(pool):
            make_identity(nc, pool, ident, made)
            nc.gpsimd.memset(half_neg[:], -0.5).then_inc(made, 1)
            nc.gpsimd.memset(b_qk[:, 0], 0.0).then_inc(bias_done, 1)
            nc.gpsimd.memset(b_v[0][:], 0.0).then_inc(bias_done, 1)
            pool.wait_ge(bias_in, 144)
            nc.gpsimd.tensor_scalar(b_qk[:, 1, 0, :], b_qk[:, 1, 0, :], -SCALE, None, ALU.mult).then_inc(bias_done, 1)
            nc.gpsimd.memset(rstd2[:], 1.0).then_inc(epi_done, 1)
            pool.wait_ge(made, 3)

            def norm(job):
                wait_apart(pool, made, mv_done, job + 1)
                nc.gpsimd.tensor_scalar(var_eps[:], mv[:, :, 1], EPS, None, ALU.add).then_inc(ln_chain, 1)
                pool.wait_ge(ln_chain, 2 * job + 1)
                nc.gpsimd.tensor_tensor(rstd[:], var_eps[:], half_neg[:], op=ALU.pow).then_inc(ln_chain, 1)
                wait_apart(pool, made, ln_chain, 2 * job + 2)
                for t in range(NT):
                    nc.gpsimd.tensor_scalar(xa[:, t, :], xa[:, t, :], mv[:, t, 0:1], rstd[:, t:t + 1],
                                            ALU.subtract, ALU.mult).then_inc(hn_done, 1)

            CHAIN = 7

            def bias_xe(job, layer, p):
                pool.wait_ge(xe_in[p % 2], 32 * job + 16 * (p // 2) + 16)
                nc.gpsimd.tensor_tensor(xe[p % 2][:], xe[p % 2][:], (beta, b_out[1])[layer][:].to_broadcast([P, 2, D]),
                                        op=ALU.add).then_inc(xe_biased, 1)

            def add_ln(job, p):
                done = CHAIN * (4 * job + p)
                wait_apart(pool, made, mv2_done, 4 * job + p + 1)
                nc.gpsimd.tensor_scalar(var2[:], mv2[:, :, 1], EPS, None, ALU.add).then_inc(epi_chain, 1)
                pool.wait_ge(epi_chain, done + 1)
                nc.gpsimd.tensor_tensor(rstd2[:], var2[:], half_neg[:, 0:2], op=ALU.pow).then_inc(epi_chain, 1)
                wait_apart(pool, made, epi_chain, done + 2)
                for i in range(2):
                    nc.gpsimd.tensor_scalar(ln[:, i, :], proj[:, i, :], mv2[:, i, 0:1], rstd2[:, i:i + 1],
                                            ALU.subtract, ALU.mult).then_inc(epi_chain, 1)
                pool.wait_ge(epi_chain, done + 4)
                nc.gpsimd.tensor_tensor(ln[:], ln[:], gamma[:].to_broadcast([P, 2, D]), op=ALU.mult).then_inc(epi_chain, 1)
                pool.wait_ge(xe_biased, 4 * job + p + 1)
                nc.gpsimd.tensor_tensor(xe[p % 2][:], xe[p % 2][:], proj[:], op=ALU.add).then_inc(epi_chain, 1)
                pool.wait_ge(epi_chain, done + 6)
                nc.gpsimd.tensor_tensor(xe[p % 2][:], xe[p % 2][:], ln[:], op=ALU.add).then_inc(epi_done, 1)
                nc.gpsimd.memset(var2[:], 0.0).then_inc(epi_chain, 1)
                pool.wait_ge(epi_chain, done + 7)

            def epilogue(job, layer):
                for p in range(4):
                    bias_xe(job, layer, p)
                    if layer == 0:
                        add_ln(job, p)

            def mask3():
                for t in range(NT):
                    pool.wait_ge(t_done, UNITS * (B - 1) + UNITS - NT + t + 1)
                    pool.dma_start(mask[:, t, :], a["adj"][t * P:(t + 1) * P, :]).then_inc(mask_in[t], 16)
                for t in range(NT):
                    pool.wait_ge(mask_in[t], 16)
                    nc.gpsimd.tensor_scalar(mask[:, t, :], mask[:, t, :], 1.0, -1.0e9, ALU.subtract, ALU.mult)\
                        .then_inc(mask3_done, 1)

            norm(0)

            def body(job, layer, before, after):
                if before is not None:
                    epilogue(job - 1, before)
                if after is not None:
                    norm(job + 1)
                if layer != after and after is not None:
                    mask3()

            jobs(pool, body)
            epilogue(JOBS - 1, 1)


def build_program(nc, a, out):
    N = a["adj"].shape[0]
    B, _, D = a["x"].shape
    x_mid = nc.dram_tensor("x_after_graph_layers", (B, N, D), F32, kind="Internal").ap()
    x_mid2 = nc.dram_tensor("x_after_layer_2", (B, N, D), F32, kind="Internal").ap()
    with nc.sbuf_tensor("mask", [P, N // P, N], F32) as mask:
        graph_phase(nc, a, x_mid, mask)
        attention_phase(nc, a, x_mid, x_mid2, out, mask)


_INS = ["x", "adj", "L0_gnn_weight", "L0_gnn_bias", "L1_gnn_weight", "L1_gnn_bias", "L2_gnn_w_qkv",
        "L2_gnn_w_proj", "L2_gnn_b_proj", "L2_gnn_ln_gamma", "L2_gnn_ln_beta", "L3_gnn_Wq", "L3_gnn_bq",
        "L3_gnn_Wk", "L3_gnn_bk", "L3_gnn_Wv", "L3_gnn_bv", "L3_gnn_Wo", "L3_gnn_bo"]


def kernel(**inputs):
    import numpy as _np
    import concourse.bacc as _bacc
    from concourse import mybir as _mybir
    from concourse.bass_utils import run_bass_kernel_spmd as _run

    nc = _bacc.Bacc("TRN2", target_bir_lowering=False, num_devices=1)
    arrays, aps = {}, {}
    for name in _INS:
        arr = _np.ascontiguousarray(inputs[name])
        arrays["in_" + name] = arr
        aps[name] = nc.dram_tensor("in_" + name, arr.shape, _mybir.dt.from_np(arr.dtype), kind="ExternalInput").ap()
    out = nc.dram_tensor("out", inputs["x"].shape, _mybir.dt.float32, kind="ExternalOutput").ap()
    build_program(nc, aps, out)
    r = _run(nc, [arrays], core_ids=[0])
    return r.results[0]["out"]
```

```python
from contextlib import ExitStack

import concourse.bass as bass
from concourse import mybir

F32 = mybir.dt.float32
F32R = mybir.dt.float32r
ALU = mybir.AluOpType
ACT = mybir.ActivationFunctionType
AX_X = mybir.AxisListType.X

P = 128
EPS = 1e-5
HEADS = 8
BIG = 3.0e38


def wait_apart(eng, begun, sem, value):
    value = value if isinstance(value, int) else eng.to_reg(value)
    eng.wait_ge(begun, 1)
    eng.wait_ge(sem, value)


def make_identity(nc, pool, ident, made):
    nc.gpsimd.memset(ident[:], 0.0).then_inc(made, 1)
    pool.wait_ge(made, 1)
    nc.gpsimd.affine_select(out=ident[:], in_=ident[:], compare_op=ALU.not_equal, fill=1.0, base=0,
                            pattern=[[-1, P]], channel_multiplier=1).then_inc(made, 1)


def graph_phase(nc, a, x_mid, mask):
    B, N, D = a["x"].shape
    NT, DC = N // P, D // P
    HALF = N // 2
    HT = HALF // P
    SLOTS = 4
    ROUNDS = B // SLOTS
    YG = 2 * DC
    with ExitStack() as ctx:
        def sb(name, shape, dt=F32):
            return ctx.enter_context(nc.sbuf_tensor("g_" + name, shape, dt))

        def sem(name):
            return ctx.enter_context(nc.semaphore("g_" + name))

        ident = sb("ident", [P, P])
        adjT_hi = sb("adjT_hi", [P, NT, N], F32R)
        adjT_lo = sb("adjT_lo", [P, NT, N], F32R)
        x_sb = [sb(f"x{i}", [P, NT, D]) for i in range(SLOTS)]
        hn = sb("hn", [P, NT, D])
        h_hi = [sb(f"h_hi{i}", [P, NT, D], F32R) for i in range(2)]
        h_lo = [sb(f"h_lo{i}", [P, NT, D], F32R) for i in range(2)]
        yT_hi = sb("yT_hi", [P, DC, N], F32R)
        yT_lo = sb("yT_lo", [P, DC, N], F32R)
        w_raw = sb("w_raw", [P, 2, DC, D])
        w_hi = sb("w_hi", [P, 2, DC, D], F32R)
        w_lo = sb("w_lo", [P, 2, DC, D], F32R)
        bias = sb("bias", [P, 2, D])
        stats = sb("stats", [P, NT, 6])
        mv = sb("mv", [P, NT, 2])
        var_eps = sb("var_eps", [P, NT])
        rstd = sb("rstd", [P, NT])
        half_neg = sb("half_neg", [P, NT])
        adj_copy = sb("adj_copy", [P, N])
        deg = sb("deg", [P, NT])
        deg_pos = sb("deg_pos", [P, NT])
        deg_floor = sb("deg_floor", [P, NT])
        deg_is = sb("deg_is", [P, NT])
        spare = sb("spare", [P, NT])
        ps = [ctx.enter_context(nc.psum_tensor(f"g_ps{i}", [P, 512], F32)) for i in range(8)]
        y_ps, w_ps = ps[:4], ps[4:]

        made = sem("made")
        adj_in = [sem(f"adj_in{i}") for i in range(2)]
        w_in = sem("w_in")
        x_in = [sem(f"x_in{i}") for i in range(SLOTS)]
        x_stored = [sem(f"x_stored{i}") for i in range(SLOTS)]
        at_mm = sem("at_mm")
        at_hi = sem("at_hi")
        at_free = sem("at_free")
        w_hi_done = sem("w_hi_done")
        w_split = sem("w_split")
        deg_done = sem("deg_done")
        r_chain = sem("r_chain")
        stat_done = sem("stat_done")
        mv_done = sem("mv_done")
        ln_chain = sem("ln_chain")
        hn_done = sem("hn_done")
        xb_done = sem("xb_done")
        relu_hi = sem("relu_hi")
        h_done = sem("h_done")
        y_mm = sem("y_mm")
        y_hi_done = sem("y_hi_done")
        y_free = sem("y_free")
        w_mm = sem("w_mm")
        w_free = sem("w_free")
        mask_done = sem("mask_done")
        block = ctx.enter_context(nc.Block())

        AT = 2 * NT

        def job_of(m):
            return m % 4 // 2, 2 * (m // 4) + m % 2, m % 2

        def x_rows(dram, batch):
            return dram[batch].rearrange("(t p) d -> p t d", p=P)

        @block.sync
        def _(sp):
            sp.dma_start(x_sb[0][:], x_rows(a["x"], 0)).then_inc(x_in[0], 16)
            for t in range(NT):
                sp.dma_start(mask[:, t, :], a["adj"][t * P:(t + 1) * P, :]).then_inc(adj_in[t // HT], 16)
            for layer, name in enumerate(("L0_gnn", "L1_gnn")):
                sp.dma_start(w_raw[:, layer], a[name + "_weight"].rearrange("(c p) o -> p c o", p=P)).then_inc(w_in, 16)
                sp.dma_start(bias[:, layer], a[name + "_bias"].partition_broadcast(P)).then_inc(w_in, 16)
            for s in range(1, SLOTS):
                sp.dma_start(x_sb[s][:], x_rows(a["x"], s)).then_inc(x_in[s], 16)
            for rnd in range(ROUNDS):
                for s in range(SLOTS):
                    job = 8 * rnd + 4 * (s // 2) + 2 + s % 2
                    sp.wait_ge(w_free, 4 * (job + 2))
                    sp.dma_start(x_rows(x_mid, SLOTS * rnd + s), x_sb[s][:]).then_inc(x_stored[s], 16)
                    if rnd + 1 < ROUNDS:
                        sp.wait_ge(x_stored[s], 16 * (rnd + 1))
                        sp.dma_start(x_sb[s][:], x_rows(a["x"], SLOTS * (rnd + 1) + s)).then_inc(x_in[s], 16)
            for s in range(SLOTS):
                sp.wait_ge(x_stored[s], 16 * ROUNDS)

        @block.tensor
        def _(pe):
            mm = nc.tensor.matmul
            pe.wait_ge(made, 2)
            for n in range(AT):
                m, nh = n % NT, n // NT
                pe.wait_ge(adj_in[nh], 16 * HT)
                if n >= 8:
                    pe.wait_ge(at_free, n - 7)
                for i in range(HT):
                    last = nc.tensor.transpose(ps[n % 8][:, i * P:(i + 1) * P],
                                               mask[:, nh * HT + i, m * P:(m + 1) * P], ident[:])
                last.then_inc(at_mm, 1)

            def split_product(out, stat, mov, first, final):
                (s_hi, s_lo), (m_hi, m_lo) = stat, mov
                mm(out, s_hi, m_hi, start=first, stop=False)
                mm(out, s_hi, m_lo, start=False, stop=False)
                return mm(out, s_lo, m_hi, start=False, stop=final)

            def y_group(job, g, s):
                nh, c = g // DC, g % DC
                pe.wait_ge(y_free, 4 * job + g + 1)
                for m in range(NT):
                    stat = (h_hi[s][:, m, c * P:(c + 1) * P], h_lo[s][:, m, c * P:(c + 1) * P])
                    mov = (adjT_hi[:, m, nh * HALF:(nh + 1) * HALF], adjT_lo[:, m, nh * HALF:(nh + 1) * HALF])
                    last = split_product(y_ps[g][:], stat, mov, m == 0, m == NT - 1)
                last.then_inc(y_mm, 1)

            def w_blocks(job, layer, qs):
                for q in qs:
                    pe.wait_ge(y_free, 4 * job + DC * (q // 2 + 1) + 4)
                    pe.wait_ge(w_free, 4 * job + q + 1)
                    for i in range(2):
                        t = 2 * q + i
                        for c in range(DC):
                            stat = (yT_hi[:, c, t * P:(t + 1) * P], yT_lo[:, c, t * P:(t + 1) * P])
                            mov = (w_hi[:, layer, c, :], w_lo[:, layer, c, :])
                            last = split_product(w_ps[q][:, i * D:(i + 1) * D], stat, mov, c == 0, c == DC - 1)
                    last.then_inc(w_mm, 1)

            pe.wait_ge(at_free, AT)
            pe.wait_ge(w_split, 1)
            with pe.Fori(0, ROUNDS) as rnd:
                for m in range(8):
                    job = 8 * rnd + m
                    layer, _, s = job_of(m)
                    pe.wait_ge(h_done, job + 1)
                    y_group(job, 0, s)
                    if m > 0:
                        w_blocks(job - 1, job_of(m - 1)[0], (2, 3))
                    y_group(job, 1, s)
                    y_group(job, 2, s)
                    w_blocks(job, layer, (0, 1))
                    y_group(job, 3, s)
                w_blocks(8 * rnd + 7, 1, (2, 3))

        @block.scalar
        def _(act):
            for n in range(AT):
                m, nh = n % NT, n // NT
                act.wait_ge(at_mm, n + 1)
                nc.scalar.activation(adjT_hi[:, m, nh * HALF:(nh + 1) * HALF], ps[n % 8][:], ACT.Copy).then_inc(at_hi, 1)
            act.wait_ge(w_in, 64)
            nc.scalar.activation(w_hi[:], w_raw[:], ACT.Copy).then_inc(w_hi_done, 1)
            for t in range(NT):
                if t:
                    act.wait_ge(deg_done, t)
                nc.scalar.activation(adj_copy[:], mask[:, t, :], ACT.Copy, accum_out=deg[:, t:t + 1]).then_inc(deg_done, 1)
            with act.Fori(0, 8 * ROUNDS) as job:
                for g in range(YG):
                    nh, c = g // DC, g % DC
                    act.wait_ge(y_mm, 4 * job + g + 1)
                    nc.scalar.activation(yT_hi[:, c, nh * HALF:(nh + 1) * HALF], y_ps[g][:], ACT.Copy).then_inc(y_hi_done, 1)

        @block.gpsimd
        def _(pool):
            make_identity(nc, pool, ident, made)
            nc.gpsimd.memset(half_neg[:], -0.5).then_inc(made, 1)
            pool.wait_ge(made, 3)
            chain = 0
            for job in range(8 * ROUNDS):
                layer, s, _ = job_of(job % 8)
                pool.wait_ge(mv_done, job + 1)
                nc.gpsimd.tensor_scalar(var_eps[:], mv[:, :, 1], EPS, None, ALU.add).then_inc(ln_chain, 1)
                pool.wait_ge(ln_chain, chain + 1)
                nc.gpsimd.tensor_tensor(rstd[:], var_eps[:], half_neg[:], op=ALU.pow).then_inc(ln_chain, 1)
                if layer:
                    pool.wait_ge(ln_chain, chain + 2)
                    nc.gpsimd.tensor_tensor(rstd[:], rstd[:], deg_is[:], op=ALU.mult).then_inc(ln_chain, 1)
                chain += 2 + layer
                if job == 1:
                    pool.wait_ge(deg_done, NT)
                    nc.gpsimd.tensor_scalar(deg_floor[:], deg[:], 1e-30, None, ALU.max).then_inc(r_chain, 1)
                    nc.gpsimd.tensor_scalar(deg_pos[:], deg[:], 0.0, None, ALU.is_gt).then_inc(r_chain, 1)
                    pool.wait_ge(r_chain, 2)
                    nc.gpsimd.tensor_tensor(deg_is[:], deg_floor[:], half_neg[:], op=ALU.pow).then_inc(r_chain, 1)
                    pool.wait_ge(r_chain, 3)
                    nc.gpsimd.tensor_tensor(deg_is[:], deg_is[:], deg_pos[:], op=ALU.mult).then_inc(r_chain, 1)
                    pool.wait_ge(r_chain, 4)
                pool.wait_ge(hn_done, job + 1)
                if job == 0:
                    pool.wait_ge(w_in, 64)
                nc.gpsimd.tensor_tensor(x_sb[s][:], x_sb[s][:],
                                        bias[:, layer:layer + 1, :].to_broadcast([P, NT, D]), op=ALU.add).then_inc(xb_done, 1)

        @block.vector
        def _(dve):
            def rstd_steps(job):
                return 2 * (job + 1) + 2 * (job // 4) + max(0, job % 4 - 1)

            def ln_stats(job):
                layer, s, _ = job_of(job % 8)
                if layer == 0:
                    dve.wait_ge(x_in[s], 16 * (job // 8 + 1))
                else:
                    dve.wait_ge(w_free, 4 * job)
                for t in range(NT):
                    nc.vector.bn_stats(stats[:, t, :], x_sb[s][:, t, :]).then_inc(stat_done, 1)
                dve.wait_ge(stat_done, 8 * job + 8)
                for t in range(NT):
                    last = nc.vector.bn_aggr(mv[:, t, :], stats[:, t, :])
                last.then_inc(mv_done, 1)

            def norm_split(job):
                _, s, b = job_of(job % 8)
                dve.wait_ge(ln_chain, rstd_steps(job))
                for t in range(NT):
                    last = nc.vector.tensor_scalar(hn[:, t, :], x_sb[s][:, t, :], mv[:, t, 0:1], rstd[:, t:t + 1],
                                                   ALU.subtract, ALU.mult)
                last.then_inc(hn_done, 1)
                dve.wait_ge(hn_done, job + 1)
                for th in range(2):
                    part = slice(th * HT, (th + 1) * HT)
                    nc.vector.tensor_scalar(h_hi[b][:, part, :], hn[:, part, :], 0.0, None, ALU.max).then_inc(relu_hi, 1)
                for th in range(2):
                    part = slice(th * HT, (th + 1) * HT)
                    dve.wait_ge(relu_hi, 2 * job + th + 1)
                    last = nc.vector.scalar_tensor_tensor(
                        out=h_lo[b][:, part, :], in0=hn[:, part, :], scalar=0.0,
                        in1=h_hi[b][:, part, :].bitcast(F32), op0=ALU.max, op1=ALU.subtract)
                last.then_inc(h_done, 1)

            def y_lo(job, g):
                nh, c = g // DC, g % DC
                dve.wait_ge(y_hi_done, 4 * job + g + 1)
                cols = slice(nh * HALF, (nh + 1) * HALF)
                nc.vector.tensor_tensor(yT_lo[:, c, cols], y_ps[g][:], yT_hi[:, c, cols].bitcast(F32),
                                        op=ALU.subtract).then_inc(y_free, 1)

            def add_out(job, qs):
                layer, s, _ = job_of(job % 8)
                dve.wait_ge(xb_done, job + 1)
                for q in qs:
                    dve.wait_ge(w_mm, 4 * job + q + 1)
                    for i in range(2):
                        t = 2 * q + i
                        last = nc.vector.scalar_tensor_tensor(
                            out=x_sb[s][:, t, :], in0=w_ps[q][:, i * D:(i + 1) * D],
                            scalar=deg_is[:, t:t + 1] if layer else 1.0, in1=x_sb[s][:, t, :],
                            op0=ALU.mult, op1=ALU.add)
                    last.then_inc(w_free, 1)

            ln_stats(0)
            norm_split(0)
            for n in range(AT):
                m, nh = n % NT, n // NT
                dve.wait_ge(at_hi, n + 1)
                cols = slice(nh * HALF, (nh + 1) * HALF)
                nc.vector.tensor_tensor(adjT_lo[:, m, cols], ps[n % 8][:], adjT_hi[:, m, cols].bitcast(F32),
                                        op=ALU.subtract).then_inc(at_free, 1)
            dve.wait_ge(w_hi_done, 1)
            nc.vector.tensor_tensor(w_lo[:], w_raw[:], w_hi[:].bitcast(F32), op=ALU.subtract).then_inc(w_split, 1)
            for t in range(NT):
                nc.vector.memset(spare[:, t:t + 1], 0.0).then_inc(y_free if t < 4 else w_free, 1)
            jobs = 8 * ROUNDS
            for job in range(jobs):
                if job % 8:
                    add_out(job - 1, (2, 3))
                y_lo(job, 0)
                if job + 1 < jobs:
                    ln_stats(job + 1)
                y_lo(job, 1)
                if job + 1 < jobs:
                    norm_split(job + 1)
                y_lo(job, 2)
                add_out(job, (0, 1))
                y_lo(job, 3)
                if job % 8 == 7:
                    add_out(job, (2, 3))
                if job == 1:
                    dve.wait_ge(deg_done, NT)
                    for t in range(NT):
                        nc.vector.tensor_scalar(mask[:, t, :], mask[:, t, :], 0.0, BIG, ALU.is_equal, ALU.mult).then_inc(mask_done, 1)
            dve.wait_ge(mask_done, NT)


UNITS = 64
EARLY = [(9, ("norm", 3)), (11, ("turn", 0)), (13, ("out", 0)), (14, ("turn", 1)), (16, ("out", 1)),
         (26, ("turn", 2)), (28, ("out", 2)), (29, ("turn", 3)), (31, ("out", 3))]
MID = [(18, ("qk", 1, 0, 0)), (20, ("qk", 1, 1, 0)), (22, ("qk", 1, 0, 1)), (24, ("qk", 1, 1, 1)),
       (33, ("norm", 0)), (46, ("norm", 1)), (60, ("norm", 2))]
NEXT = [(35, ("h", 0, 0)), (37, ("h", 0, 1)), (38, ("h", 1, 0)), (41, ("h", 1, 1)),
        (42, ("v", 0)), (44, ("v", 1)), (47, ("v", 2)), (49, ("v", 3)),
        (51, ("qk", 0, 0, 0)), (53, ("qk", 0, 1, 0)), (54, ("qk", 0, 0, 1)), (56, ("qk", 0, 1, 1))]
LN_STEP = 16
PER_JOB = len(EARLY) + len(MID) + len(NEXT)


def blocks_of(first, core, more):
    table = sorted((EARLY if not first else []) + (MID if core else []) + (NEXT if more else []))
    skip = len(EARLY) if first else 0
    return {step: (skip + i, what) for i, (step, what) in enumerate(table)}


def scalar_halves(table):
    return {u for u in range(UNITS)
            if (table[u][1][0] in ("v", "norm", "out") if u in table else u % 4 == 3)}


def attention_phase(nc, a, x_mid, x_mid2, out, mask):
    B, N, D = a["x"].shape
    NT, DC = N // P, D // P
    HD = D // HEADS
    HALF = N // 2
    HT = HALF // P
    JOBS = 2 * B
    SCALE = float(HD) ** -0.5
    GH = P // HD
    RING = 4
    XE = 3
    with ExitStack() as ctx:
        def sb(name, shape, dt=F32):
            return ctx.enter_context(nc.sbuf_tensor("t_" + name, shape, dt))

        def sem(name):
            return ctx.enter_context(nc.semaphore("t_" + name))

        def pb(name, width):
            return ctx.enter_context(nc.psum_tensor("t_" + name, [P, width], F32))

        ident = sb("ident", [P, P])
        w_hi = [sb(f"w_hi{i}", [P, DC, 4 * D], F32R) for i in range(2)]
        w_lo = [sb(f"w_lo{i}", [P, DC, 4 * D], F32R) for i in range(2)]
        b_qk = sb("b_qk", [P, 2, 2, 2])
        b_v = sb("b_v", [P, 1, D])
        b_out = [sb(f"b_out{i}", [P, 1, D]) for i in range(2)]
        gamma = sb("gamma", [P, 1, D])
        beta = sb("beta", [P, 1, D])
        xa = sb("xa", [P, NT, D])
        hT_hi = sb("hT_hi", [P, DC, N], F32R)
        hT_lo = sb("hT_lo", [P, DC, N], F32R)
        st_hi = [sb(f"st_hi{i}", [P, N], F32R) for i in range(2)]
        st_lo = [sb(f"st_lo{i}", [P, N], F32R) for i in range(2)]
        q4 = [sb(f"q4_{i}", [P, N], F32R) for i in range(2)]
        k4 = [sb(f"k4_{i}", [P, N], F32R) for i in range(2)]
        v_sb = sb("v", [P, NT, D])
        T = [sb(f"T{i}", [P, N]) for i in range(RING)]
        PT = sb("PT", [P, NT, NT, P])
        low = sb("low", [P, RING])
        rsum = sb("rsum", [P, UNITS])
        rinv = sb("rinv", [P, UNITS])
        ot_sb = sb("ot", [P, 512])
        o_sb = sb("o", [P, NT, D])
        oT_hi = sb("oT_hi", [P, 512], F32R)
        oT_lo = sb("oT_lo", [P, 512], F32R)
        xe = [sb(f"xe{i}", [P, 2, D]) for i in range(XE)]
        proj = [sb(f"proj{i}", [P, 2, D]) for i in range(2)]
        stats = sb("stats", [P, NT, 6])
        mv = sb("mv", [P, NT, 2])
        var_eps = sb("var_eps", [P, NT])
        rstd = sb("rstd", [P, NT])
        half_neg = sb("half_neg", [P, NT])
        stats2 = [sb(f"stats2_{i}", [P, 2, 6]) for i in range(2)]
        mv2 = [sb(f"mv2_{i}", [P, 2, 2]) for i in range(2)]
        var2 = sb("var2", [P, 2])
        rstd2 = [sb(f"rstd2_{i}", [P, 2]) for i in range(2)]
        spare = sb("spare", [P, 4])

        s_ps = [pb(f"s_ps{i}", N) for i in range(2)]
        pt_ps = [pb(f"pt_ps{i}", 512) for i in range(2)]
        ot_ps = pb("ot_ps", 512)
        g_ps = pb("g_ps", 512)

        made = sem("made")
        raw_in = [sem(f"raw_in{i}") for i in range(2)]
        bias_in = sem("bias_in")
        bias_done = sem("bias_done")
        w_hi_done = sem("w_hi_done")
        w_split = sem("w_split")
        xa_in = sem("xa_in")
        stat_done = sem("stat_done")
        mv_done = sem("mv_done")
        ln_chain = sem("ln_chain")
        hn_done = sem("hn_done")
        g_mm = sem("g_mm")
        g_free = sem("g_free")
        h_hi_done = sem("h_hi_done")
        qk_hi_done = sem("qk_hi_done")
        oT_hi_done = sem("oT_hi_done")
        head_in = [sem(f"head_in{i}") for i in range(2)]
        s_done = sem("s_done")
        t_done = sem("t_done")
        p_done = sem("p_done")
        tr_done = [sem(f"tr_done{i}") for i in range(2)]
        pt_done = [sem(f"pt_done{i}") for i in range(2)]
        av_done = sem("av_done")
        ot_done = sem("ot_done")
        rinv_done = sem("rinv_done")
        xe_in = [sem(f"xe_in{i}") for i in range(4)]
        v_moved = sem("v_moved")
        xe_biased = sem("xe_biased")
        x_stored = sem("x_stored")
        stat2_done = sem("stat2_done")
        mv2_done = sem("mv2_done")
        var2_done = sem("var2_done")
        rstd2_done = sem("rstd2_done")
        proj_added = sem("proj_added")
        centered = sem("centered")
        ln2_chain = sem("ln2_chain")
        epi_done = sem("epi_done")
        mask_in = [sem(f"mask_in{t}") for t in range(NT)]
        mask3_done = sem("mask3_done")
        block = ctx.enter_context(nc.Block())

        FIRST_BLOCKS = len(NEXT)

        def block_at(job, k):
            return PER_JOB * job + FIRST_BLOCKS - len(EARLY) + k

        def jobs(eng, body):
            body(0, 0, None, 0)
            with eng.Fori(1, B - 1) as job:
                body(job, 0, 0, 0)
            body(B - 1, 0, 0, 1)
            body(B, 1, 0, 1)
            with eng.Fori(B + 1, JOBS - 1) as job:
                body(job, 1, 1, 1)
            body(JOBS - 1, 1, 1, None)

        def tail_block(k):
            return block_at(JOBS, k) - len(NEXT)

        def raw_weights(layer):
            width = DC * 4 * D
            return PT[:].rearrange("p a b c -> p (a b c)")[:, layer * width:(layer + 1) * width]\
                .rearrange("p (c o) -> p c o", c=DC)

        def pt_of(u, half):
            qt, keys = u % NT, slice(half * HT, (half + 1) * HT)
            return PT[:, qt, keys, :] if u // NT % 2 == 0 else PT[:, keys, qt, :]

        def x_of(layer, batch):
            return (x_mid, x_mid2)[layer][batch]

        @block.sync
        def _(sp):
            sp.dma_start(xa[:], x_of(0, 0).rearrange("(t p) d -> p t d", p=P)).then_inc(xa_in, 16)
            raw = [raw_weights(i) for i in range(2)]
            sp.dma_start(raw[0][:, :, 0:3 * D], a["L2_gnn_w_qkv"].rearrange("(c p) o -> p c o", p=P)).then_inc(raw_in[0], 16)
            sp.dma_start(raw[0][:, :, 3 * D:], a["L2_gnn_w_proj"].rearrange("(c p) o -> p c o", p=P)).then_inc(raw_in[0], 16)
            for i, name in enumerate(("Wq", "Wk", "Wv", "Wo")):
                sp.dma_start(raw[1][:, :, i * D:(i + 1) * D],
                             a["L3_gnn_" + name].rearrange("(c p) o -> p c o", p=P)).then_inc(raw_in[1], 16)
            for dst, name in ((b_v, "L3_gnn_bv"), (b_out[0], "L2_gnn_b_proj"), (b_out[1], "L3_gnn_bo"),
                              (gamma, "L2_gnn_ln_gamma"), (beta, "L2_gnn_ln_beta")):
                sp.dma_start(dst[:, 0, :], a[name].partition_broadcast(P)).then_inc(bias_in, 16)
            for w, name in enumerate(("L3_gnn_bq", "L3_gnn_bk")):
                for g in range(2):
                    sp.dma_start(b_qk[:, 1, w, g:g + 1], a[name][g * P:(g + 1) * P].rearrange("(p o) -> p o", o=1)).then_inc(bias_in, 16)

            def load_head(job, h, slot_free, staged):
                s, rows = h % 2, slice((h % GH) * HD, (h % GH + 1) * HD)
                if slot_free is not None:
                    wait_apart(sp, raw_in[0], s_done, slot_free)
                if staged is not None:
                    sp.wait_ge(g_free, staged)
                for part in range(4):
                    dst = slice(part * HD, (part + 1) * HD)
                    sp.dma_start(q4[s][dst, :].bitcast(F32), (st_hi, st_lo)[part // 2][0][rows, :].bitcast(F32)).then_inc(head_in[s], 16)
                    sp.dma_start(k4[s][dst, :].bitcast(F32), (st_hi, st_lo)[part % 2][1][rows, :].bitcast(F32)).then_inc(head_in[s], 16)

            def load_xe(job, layer, p):
                batch = job - B * layer
                sp.dma_start(xe[p % XE][:], x_of(layer, batch)[2 * p * P:2 * (p + 1) * P, :]
                             .rearrange("(t p) d -> p t d", p=P)).then_inc(xe_in[p], 16)

            def store(job, layer, p, n):
                batch = job - B * layer
                if layer == 0:
                    wait_apart(sp, raw_in[0], epi_done, 4 * job + p + 3)
                else:
                    wait_apart(sp, raw_in[0], g_free, n + 1)
                sp.dma_start((x_mid2, out)[layer][batch, 2 * p * P:2 * (p + 1) * P, :]
                             .rearrange("(t p) d -> p t d", p=P), xe[p % XE][:]).then_inc(x_stored, 16)

            def after_store(job, p):
                wait_apart(sp, raw_in[0], x_stored, 16 * (4 * job + p + 1))

            def body(job, layer, before, after):
                table = blocks_of(before is None, True, after is not None)
                at = {what: block_at(job, k) for k, what in table.values()}
                if before is not None:
                    for p in range(XE):
                        load_xe(job - 1, before, p)
                if after is not None:
                    wait_apart(sp, raw_in[0], v_moved, job + 1)
                    sp.dma_start(xa[:], x_of(after, job + 1 - B * after).rearrange("(t p) d -> p t d", p=P)).then_inc(xa_in, 16)
                load_head(job, 2, UNITS * job + 8, None)
                load_head(job, 3, UNITS * job + 16, None)
                if before is not None:
                    store(job - 1, before, 0, at[("out", 0)])
                    after_store(job - 1, 0)
                    load_xe(job - 1, before, 3)
                    store(job - 1, before, 1, at[("out", 1)])
                load_head(job, 4, UNITS * job + 24, at[("qk", 1, 1, 1)] + 1)
                if before is not None:
                    store(job - 1, before, 2, at[("out", 2)])
                load_head(job, 5, UNITS * job + 32, None)
                if before is not None:
                    store(job - 1, before, 3, at[("out", 3)])
                load_head(job, 6, UNITS * job + 40, None)
                load_head(job, 7, UNITS * job + 48, None)
                if before is not None:
                    after_store(job - 1, 3)
                if after is not None:
                    load_head(job + 1, 0, UNITS * job + 56, at[("qk", 0, 1, 1)] + 1)
                    load_head(job + 1, 1, UNITS * job + 64, None)

            load_head(0, 0, None, FIRST_BLOCKS)
            load_head(0, 1, None, None)
            jobs(sp, body)
            table = blocks_of(False, False, False)
            at = {what: tail_block(k) for k, what in table.values()}
            for p in range(XE):
                load_xe(JOBS - 1, 1, p)
            for p in range(4):
                store(JOBS - 1, 1, p, at[("out", p)])
                if p == 0:
                    after_store(JOBS - 1, p)
                    load_xe(JOBS - 1, 1, XE)
            after_store(JOBS - 1, 3)

        @block.tensor
        def _(pe):
            mm = nc.tensor.matmul

            def split_product(dst, stat, mov, first, final):
                (s_hi, s_lo), (m_hi, m_lo) = stat, mov
                mm(dst, s_hi, m_hi, start=first, stop=False)
                mm(dst, s_hi, m_lo, start=False, stop=False)
                return mm(dst, s_lo, m_hi, start=False, stop=final)

            def scores(job, u, wait):
                job, u = (job + 1, u - UNITS) if u >= UNITS else (job, u)
                h, qt = u // NT, u % NT
                if qt == 0:
                    pe.wait_ge(head_in[h % 2], 128 * (4 * job + h // 2 + 1))
                if wait is not None:
                    pe.wait_ge(t_done, wait)
                for half in range(2):
                    cols = slice(half * HALF, (half + 1) * HALF)
                    last = mm(s_ps[u % 2][:, cols], q4[h % 2][:, qt * P:(qt + 1) * P], k4[h % 2][:, cols],
                              start=True, stop=True)
                last.then_inc(s_done, 1)

            def transposes(job, u):
                pe.wait_ge(p_done, UNITS * job + u + 1)
                for half in range(2):
                    pe.wait_ge(pt_done[half], UNITS * job + u + 1)
                    for i in range(HT):
                        kt = half * HT + i
                        last = nc.tensor.transpose(pt_ps[half][:, i * P:(i + 1) * P],
                                                   T[u % RING][:, kt * P:(kt + 1) * P], ident[:])
                    last.then_inc(tr_done[half], 1)

            def values(job, u):
                h, kt = u // NT - 1 if u >= NT else HEADS - 1, u % NT
                if kt % HT == 0:
                    pe.wait_ge(pt_done[kt // HT], UNITS * job + u - kt + 1)
                if kt == 0 and h == HEADS // 2:
                    pe.wait_ge(v_moved, job + 1)
                if kt == 0 and h % 2 == 0 and not (isinstance(job, int) and job == 0 and h == 0):
                    pe.wait_ge(ot_done, 4 * job + h // 2)
                for j in range(HT):
                    probs = PT[:, j:NT:HT, kt, :] if h % 2 == 0 else PT[:, kt, j:NT:HT, :]
                    last = mm(ot_ps[j * HD:(j + 1) * HD, h % 2 * 2 * P:(h % 2 + 1) * 2 * P],
                              v_sb[:, kt, h * HD:(h + 1) * HD], probs, start=kt == 0, stop=kt == NT - 1)
                last.then_inc(av_done, 1)

            def one_block(n, what, layer, job_of_h):
                if not (isinstance(n, int) and n == 0):
                    pe.wait_ge(g_free, n)
                kind = what[0]
                if kind == "norm":
                    for i in range(4):
                        last = nc.tensor.transpose(g_ps[:, i * P:(i + 1) * P], ot_sb[:, i * P:(i + 1) * P], ident[:])
                elif kind == "turn":
                    for i in range(4):
                        t, c = 2 * what[1] + i // DC, i % DC
                        last = nc.tensor.transpose(g_ps[:, i * P:(i + 1) * P], o_sb[:, t, c * P:(c + 1) * P], ident[:])
                elif kind == "out":
                    for i in range(2):
                        for c in range(DC):
                            at = slice((DC * i + c) * P, (DC * i + c + 1) * P)
                            cols = slice(3 * D, 4 * D)
                            last = split_product(g_ps[:, i * D:(i + 1) * D], (oT_hi[:, at], oT_lo[:, at]),
                                                 (w_hi[layer][:, c, cols], w_lo[layer][:, c, cols]), c == 0, c == DC - 1)
                elif kind == "h":
                    c, nh = what[1:]
                    pe.wait_ge(hn_done, 4 * job_of_h + 2 * nh + 2)
                    for i in range(HT):
                        last = nc.tensor.transpose(g_ps[:, i * P:(i + 1) * P],
                                                   xa[:, nh * HT + i, c * P:(c + 1) * P], ident[:])
                elif kind == "qk":
                    g, w, nh = what[1:]
                    cols, toks = slice(w * D + g * P, w * D + (g + 1) * P), slice(nh * HALF, (nh + 1) * HALF)
                    for c in range(DC):
                        last = split_product(g_ps[:], (w_hi[layer][:, c, cols], w_lo[layer][:, c, cols]),
                                             (hT_hi[:, c, toks], hT_lo[:, c, toks]), c == 0, c == DC - 1)
                else:
                    cols = slice(2 * D, 3 * D)
                    for i in range(2):
                        toks = slice((2 * what[1] + i) * P, (2 * what[1] + i + 1) * P)
                        for c in range(DC):
                            last = split_product(g_ps[:, i * D:(i + 1) * D], (hT_hi[:, c, toks], hT_lo[:, c, toks]),
                                                 (w_hi[layer][:, c, cols], w_lo[layer][:, c, cols]), c == 0, c == DC - 1)
                last.then_inc(g_mm, 1)

            def body(job, layer, before, after):
                table = blocks_of(before is None, True, after is not None)
                for u in range(UNITS):
                    if u + 2 < UNITS or after is not None:
                        scores(job, u + 2, UNITS * job + u + 1)
                    if u in table:
                        k, what = table[u]
                        lay = before if (u, what) in EARLY else after if (u, what) in NEXT else layer
                        if what[0] == "norm":
                            pe.wait_ge(ot_done, 4 * job + what[1] + 1 if what[1] < 3 else 4 * job)
                        one_block(block_at(job, k), what, lay, job + 1)
                    if u >= NT or before is not None:
                        values(job, u)
                    transposes(job, u)

            pe.wait_ge(made, 3)
            for n, (_, what) in enumerate(NEXT):
                if n == 4:
                    pe.wait_ge(w_split, 1)
                one_block(n, what, 0, 0)
            pe.wait_ge(w_split, 2)
            scores(0, 0, None)
            scores(0, 1, None)
            jobs(pe, body)
            for u in range(NT):
                values(JOBS, u)
            for k, what in blocks_of(False, False, False).values():
                if what[0] == "norm":
                    pe.wait_ge(ot_done, 4 * JOBS)
                one_block(tail_block(k), what, 1, None)

        @block.scalar
        def _(act):
            copy = nc.scalar.activation

            def hi_part(n, what, layer, job):
                kind = what[0]
                if kind == "h":
                    c, nh = what[1:]
                    act.wait_ge(g_mm, n + 1)
                    copy(hT_hi[:, c, nh * HALF:(nh + 1) * HALF], g_ps[:], ACT.Relu).then_inc(h_hi_done, 1)
                elif kind == "qk":
                    g, w, nh = what[1:]
                    if not (g == 0 and isinstance(job, int) and job == 0):
                        for s in range(2):
                            act.wait_ge(head_in[s], 128 * (4 * job + 2 * g))
                    act.wait_ge(g_mm, n + 1)
                    copy(st_hi[w][:, nh * HALF:(nh + 1) * HALF], g_ps[:], ACT.Identity,
                         bias=b_qk[:, layer, w, g:g + 1]).then_inc(qk_hi_done, 1)
                elif kind == "turn":
                    act.wait_ge(g_mm, n + 1)
                    copy(oT_hi[:], g_ps[:], ACT.Copy).then_inc(oT_hi_done, 1)

            def exp(job, u):
                job, u = (job + 1, u - UNITS) if u >= UNITS else (job, u)
                act.wait_ge(t_done, UNITS * job + u + 1)
                nc.scalar.activation(T[u % RING][:], T[u % RING][:], ACT.Exp, bias=low[:, u % RING:u % RING + 1],
                                     scale=-1.0, accum_out=rsum[:, u:u + 1]).then_inc(p_done, 1)

            def copy_pt(job, u, half):
                act.wait_ge(tr_done[half], UNITS * job + u + 1)
                copy(pt_of(u, half),
                     pt_ps[half][:].rearrange("p (k q) -> p k q", k=HT), ACT.Copy).then_inc(pt_done[half], 1)

            def copy_ot(after):
                act.wait_ge(av_done, after)
                copy(ot_sb[:], ot_ps[:], ACT.Copy).then_inc(ot_done, 1)

            def weights_hi(layer):
                act.wait_ge(raw_in[layer], (32, 64)[layer])
                raw = raw_weights(layer)
                copy(w_hi[layer][:, :, 0:D], raw[:, :, 0:D], ACT.Copy, scale=-SCALE).then_inc(w_hi_done, 1)
                copy(w_hi[layer][:, :, D:], raw[:, :, D:], ACT.Copy).then_inc(w_hi_done, 1)

            weights_hi(0)
            act.wait_ge(bias_done, 2)
            for n, (_, what) in enumerate(NEXT):
                hi_part(n, what, 0, 0)
                if n == 3:
                    weights_hi(1)
            exp(0, 0)

            def body(job, layer, before, after):
                table = blocks_of(before is None, True, after is not None)
                for u in range(UNITS):
                    if u + 1 < UNITS or after is not None:
                        exp(job, u + 1)
                    if u % (2 * NT) == NT - 1 and (u >= NT or before is not None):
                        copy_ot(UNITS * job + u + 1 - NT)
                    if u in table:
                        k, what = table[u]
                        in_next = (u, what) in NEXT
                        hi_part(block_at(job, k), what, after if in_next else layer, job + 1 if in_next else job)
                    copy_pt(job, u, 0)
                    if u in scalar_halves(table):
                        copy_pt(job, u, 1)

            jobs(act, body)
            copy_ot(UNITS * JOBS)
            for k, what in blocks_of(False, False, False).values():
                hi_part(tail_block(k), what, 1, None)

        @block.vector
        def _(dve):
            def masked(job, u, layer):
                job, u = (job + 1, u - UNITS) if u >= UNITS else (job, u)
                qt = u % NT
                if layer == 1 and isinstance(job, int) and job == B:
                    dve.wait_ge(mask3_done, qt + 1)
                wait_apart(dve, made, s_done, UNITS * job + u + 1)
                nc.vector.tensor_tensor_reduce(out=T[u % RING][:], in0=s_ps[u % 2][:], in1=mask[:, qt, :],
                                               scale=1.0, scalar=3.4e38, op0=ALU.add, op1=ALU.min,
                                               accum_out=low[:, u % RING:u % RING + 1]).then_inc(t_done, 1)

            def finish_block(n, what, layer, job):
                kind = what[0]
                if kind == "h":
                    c, nh = what[1:]
                    cols = slice(nh * HALF, (nh + 1) * HALF)
                    dve.wait_ge(h_hi_done, 4 * job + 2 * c + nh + 1)
                    nc.vector.scalar_tensor_tensor(out=hT_lo[:, c, cols], in0=g_ps[:], scalar=0.0,
                                                   in1=hT_hi[:, c, cols].bitcast(F32),
                                                   op0=ALU.max, op1=ALU.subtract).then_inc(g_free, 1)
                elif kind == "qk":
                    g, w, nh = what[1:]
                    cols = slice(nh * HALF, (nh + 1) * HALF)
                    dve.wait_ge(qk_hi_done, 8 * job + 4 * g + 2 * nh + w + 1)
                    nc.vector.scalar_tensor_tensor(out=st_lo[w][:, cols], in0=g_ps[:], scalar=b_qk[:, layer, w, g:g + 1],
                                                   in1=st_hi[w][:, cols].bitcast(F32),
                                                   op0=ALU.add, op1=ALU.subtract).then_inc(g_free, 1)
                elif kind == "v":
                    tiles = slice(2 * what[1], 2 * what[1] + 2)
                    dve.wait_ge(g_mm, n + 1)
                    for g, dst in enumerate((v_sb, xa)):
                        src = g_ps[:].rearrange("p (t d) -> p t d", t=2)[:, :, g * P:(g + 1) * P]
                        if layer == 0:
                            last = nc.vector.tensor_copy(dst[:, tiles, 0:P], src)
                        else:
                            last = nc.vector.tensor_tensor(dst[:, tiles, 0:P], src,
                                                           b_v[:, :, g * P:(g + 1) * P].to_broadcast([P, 2, P]),
                                                           op=ALU.add)
                    last.then_inc(g_free, 1)
                elif kind == "norm":
                    pr = what[1]
                    cols = slice(16 * pr, 16 * pr + 16)
                    dve.wait_ge(g_mm, n + 1)
                    nc.vector.reciprocal(rinv[:, cols], rsum[:, cols]).then_inc(rinv_done, 1)
                    dve.wait_ge(rinv_done, 4 * job + pr + 1)
                    nc.vector.tensor_tensor(
                        o_sb[:, :, 2 * pr * HD:(2 * pr + 2) * HD].rearrange("p t (h d) -> p h t d", h=2),
                        g_ps[:].rearrange("p (h t d) -> p h t d", h=2, t=NT),
                        rinv[:, cols].rearrange("p (h t o) -> p h t o", h=2, o=1).to_broadcast([P, 2, NT, HD]),
                        op=ALU.mult).then_inc(g_free, 1)
                elif kind == "turn":
                    dve.wait_ge(oT_hi_done, 4 * job + what[1] + 1)
                    nc.vector.tensor_tensor(oT_lo[:], g_ps[:], oT_hi[:].bitcast(F32), op=ALU.subtract).then_inc(g_free, 1)
                elif layer == 0:
                    p = what[1]
                    b = p % 2
                    dve.wait_ge(epi_done, 4 * job + p + 1)
                    dve.wait_ge(g_mm, n + 1)
                    nc.vector.tensor_tensor(proj[b][:], g_ps[:].rearrange("p (t d) -> p t d", t=2),
                                            b_out[0][:].to_broadcast([P, 2, D]), op=ALU.add).then_inc(g_free, 1)
                    dve.wait_ge(g_free, n + 1)
                    for i in range(2):
                        nc.vector.bn_stats(stats2[b][:, i, :], proj[b][:, i, :]).then_inc(stat2_done, 1)
                    wait_apart(dve, made, stat2_done, 8 * job + 2 * p + 2)
                    for i in range(2):
                        last = nc.vector.bn_aggr(mv2[b][:, i, :], stats2[b][:, i, :])
                    last.then_inc(mv2_done, 1)
                else:
                    p = what[1]
                    dve.wait_ge(xe_biased, 4 * job + p + 1)
                    dve.wait_ge(g_mm, n + 1)
                    nc.vector.tensor_tensor(xe[p % XE][:], g_ps[:].rearrange("p (t d) -> p t d", t=2),
                                            xe[p % XE][:], op=ALU.add).then_inc(g_free, 1)

            def copy_pt(job, u):
                dve.wait_ge(tr_done[1], UNITS * job + u + 1)
                nc.vector.tensor_copy(pt_of(u, 1),
                                      pt_ps[1][:].rearrange("p (k q) -> p k q", k=HT)).then_inc(pt_done[1], 1)

            def ln_stats(job, t):
                if t == 0:
                    dve.wait_ge(xa_in, 16 * job + 16)
                nc.vector.bn_stats(stats[:, t, :], xa[:, t, :]).then_inc(stat_done, 1)

            def ln_mean(job):
                wait_apart(dve, made, stat_done, 8 * job + 8)
                for t in range(NT):
                    last = nc.vector.bn_aggr(mv[:, t, :], stats[:, t, :])
                last.then_inc(mv_done, 1)

            def weights_lo(layer):
                raw = raw_weights(layer)
                dve.wait_ge(w_hi_done, 2 * layer + 2)
                nc.vector.scalar_tensor_tensor(out=w_lo[layer][:, :, 0:D], in0=raw[:, :, 0:D], scalar=-SCALE,
                                               in1=w_hi[layer][:, :, 0:D].bitcast(F32), op0=ALU.mult, op1=ALU.subtract)
                nc.vector.tensor_tensor(w_lo[layer][:, :, D:], raw[:, :, D:], w_hi[layer][:, :, D:].bitcast(F32),
                                        op=ALU.subtract).then_inc(w_split, 1)

            for t in range(NT):
                ln_stats(0, t)
            ln_mean(0)
            weights_lo(0)
            wait_apart(dve, made, ln_chain, 2)
            for t in range(NT):
                last = nc.vector.tensor_scalar(xa[:, t, :], xa[:, t, :], mv[:, t, 0:1], rstd[:, t:t + 1],
                                               ALU.subtract, ALU.mult)
                if t % 2 == 1:
                    last.then_inc(hn_done, 1)
            dve.wait_ge(bias_done, 2)
            for n, (_, what) in enumerate(NEXT):
                finish_block(n, what, 0, 0)
                if n == 7:
                    weights_lo(1)
            for half in range(2):
                nc.vector.memset(spare[:, half:half + 1], 0.0).then_inc(pt_done[half], 1)
            masked(0, 0, 0)
            masked(0, 1, 0)

            def body(job, layer, before, after):
                table = blocks_of(before is None, True, after is not None)
                for u in range(UNITS):
                    if u + 2 < UNITS or after is not None:
                        masked(job, u + 2, layer if u + 2 < UNITS else after)
                    if u in table:
                        k, what = table[u]
                        early, in_next = (u, what) in EARLY, (u, what) in NEXT
                        finish_block(block_at(job, k), what, before if early else after if in_next else layer,
                                     job - 1 if early else job + 1 if in_next else job)
                    if u not in scalar_halves(table):
                        copy_pt(job, u)
                    if after is not None:
                        if LN_STEP <= u < LN_STEP + NT:
                            ln_stats(job + 1, u - LN_STEP)
                        if u == LN_STEP + NT:
                            ln_mean(job + 1)

            jobs(dve, body)
            for k, what in blocks_of(False, False, False).values():
                finish_block(tail_block(k), what, 1, JOBS - 1)

        @block.gpsimd
        def _(pool):
            make_identity(nc, pool, ident, made)
            nc.gpsimd.memset(half_neg[:], -0.5).then_inc(made, 1)
            nc.gpsimd.memset(b_qk[:, 0], 0.0).then_inc(bias_done, 1)
            pool.wait_ge(bias_in, 144)
            nc.gpsimd.tensor_scalar(b_qk[:, 1, 0, :], b_qk[:, 1, 0, :], -SCALE, None, ALU.mult).then_inc(bias_done, 1)
            pool.wait_ge(made, 3)

            def row_scale(job):
                wait_apart(pool, made, mv_done, job + 1)
                nc.gpsimd.tensor_scalar(var_eps[:], mv[:, :, 1], EPS, None, ALU.add).then_inc(ln_chain, 1)
                pool.wait_ge(ln_chain, 2 * job + 1)
                nc.gpsimd.tensor_tensor(rstd[:], var_eps[:], half_neg[:], op=ALU.pow).then_inc(ln_chain, 1)

            def move_v(job):
                wait_apart(pool, made, g_free, FIRST_BLOCKS if isinstance(job, int) and job == 0 else block_at(job, 0))
                if not (isinstance(job, int) and job == 0):
                    wait_apart(pool, made, av_done, UNITS * job)
                nc.gpsimd.tensor_copy(v_sb[:, :, P:2 * P], xa[:, :, 0:P]).then_inc(v_moved, 1)

            def bias_xe(job, layer, p):
                pool.wait_ge(xe_in[p], 16 * (job + 1))
                nc.gpsimd.tensor_tensor(xe[p % XE][:], xe[p % XE][:], (beta, b_out[1])[layer][:].to_broadcast([P, 2, D]),
                                        op=ALU.add).then_inc(xe_biased, 1)

            def add_ln(job, p):
                b = p % 2
                wait_apart(pool, made, mv2_done, 4 * job + p + 1)
                nc.gpsimd.tensor_scalar(var2[:], mv2[b][:, :, 1], EPS, None, ALU.add).then_inc(var2_done, 1)
                pool.wait_ge(xe_biased, 4 * job + p + 1)
                nc.gpsimd.tensor_tensor(xe[p % XE][:], xe[p % XE][:], proj[b][:], op=ALU.add).then_inc(proj_added, 1)
                pool.wait_ge(proj_added, 4 * job + p + 1)
                nc.gpsimd.tensor_tensor(proj[b][:], proj[b][:], mv2[b][:, :, 0:1].to_broadcast([P, 2, D]),
                                        op=ALU.subtract).then_inc(ln2_chain, 1)
                pool.wait_ge(var2_done, 4 * job + p + 1)
                nc.gpsimd.tensor_tensor(rstd2[b][:], var2[:], half_neg[:, 0:2], op=ALU.pow).then_inc(rstd2_done, 1)
                pool.wait_ge(ln2_chain, 3 * (4 * job + p) + 1)
                nc.gpsimd.tensor_tensor(proj[b][:], proj[b][:], gamma[:].to_broadcast([P, 2, D]),
                                        op=ALU.mult).then_inc(ln2_chain, 1)
                pool.wait_ge(ln2_chain, 3 * (4 * job + p) + 2)
                pool.wait_ge(rstd2_done, 4 * job + p + 1)
                nc.gpsimd.tensor_tensor(proj[b][:], proj[b][:],
                                        rstd2[b][:].rearrange("p (t o) -> p t o", o=1).to_broadcast([P, 2, D]),
                                        op=ALU.mult).then_inc(ln2_chain, 1)
                pool.wait_ge(ln2_chain, 3 * (4 * job + p) + 3)
                nc.gpsimd.tensor_tensor(xe[p % XE][:], xe[p % XE][:], proj[b][:], op=ALU.add).then_inc(epi_done, 1)

            def norm(job):
                pool.wait_ge(ln_chain, 2 * job + 2)
                for p in range(NT // 2):
                    tiles = slice(2 * p, 2 * p + 2)
                    nc.gpsimd.tensor_tensor(xa[:, tiles, :], xa[:, tiles, :], mv[:, tiles, 0:1].to_broadcast([P, 2, D]),
                                            op=ALU.subtract).then_inc(centered, 1)
                    pool.wait_ge(centered, 4 * job + p - 3)
                    nc.gpsimd.tensor_tensor(xa[:, tiles, :], xa[:, tiles, :],
                                            rstd[:, tiles].rearrange("p (t o) -> p t o", o=1).to_broadcast([P, 2, D]),
                                            op=ALU.mult).then_inc(hn_done, 1)

            def mask3():
                for t in range(NT):
                    pool.wait_ge(t_done, UNITS * (B - 1) + UNITS - NT + t + 1)
                    pool.dma_start(mask[:, t, :], a["adj"][t * P:(t + 1) * P, :]).then_inc(mask_in[t], 16)
                for t in range(NT):
                    pool.wait_ge(mask_in[t], 16)
                    nc.gpsimd.tensor_scalar(mask[:, t, :], mask[:, t, :], 1.0, -1.0e9, ALU.subtract, ALU.mult)\
                        .then_inc(mask3_done, 1)

            row_scale(0)
            for b in range(2):
                nc.gpsimd.memset(spare[:, 2 + b:3 + b], 0.0).then_inc(epi_done, 1)

            def body(job, layer, before, after):
                move_v(job)
                if before is not None:
                    for p in range(XE):
                        bias_xe(job - 1, before, p)
                    if before == 0:
                        add_ln(job - 1, 0)
                        add_ln(job - 1, 1)
                    bias_xe(job - 1, before, XE)
                if after is not None:
                    row_scale(job + 1)
                    norm(job + 1)
                if before == 0:
                    add_ln(job - 1, 2)
                    add_ln(job - 1, 3)
                if layer != after and after is not None:
                    mask3()

            jobs(pool, body)
            for p in range(4):
                bias_xe(JOBS - 1, 1, p)


def build_program(nc, a, out):
    N = a["adj"].shape[0]
    B, _, D = a["x"].shape
    x_mid = nc.dram_tensor("x_after_graph_layers", (B, N, D), F32, kind="Internal").ap()
    x_mid2 = nc.dram_tensor("x_after_layer_2", (B, N, D), F32, kind="Internal").ap()
    with nc.sbuf_tensor("mask", [P, N // P, N], F32) as mask:
        graph_phase(nc, a, x_mid, mask)
        attention_phase(nc, a, x_mid, x_mid2, out, mask)


_INS = ["x", "adj", "L0_gnn_weight", "L0_gnn_bias", "L1_gnn_weight", "L1_gnn_bias", "L2_gnn_w_qkv",
        "L2_gnn_w_proj", "L2_gnn_b_proj", "L2_gnn_ln_gamma", "L2_gnn_ln_beta", "L3_gnn_Wq", "L3_gnn_bq",
        "L3_gnn_Wk", "L3_gnn_bk", "L3_gnn_Wv", "L3_gnn_bv", "L3_gnn_Wo", "L3_gnn_bo"]


def kernel(**inputs):
    import numpy as _np
    import concourse.bacc as _bacc
    from concourse import mybir as _mybir
    from concourse.bass_utils import run_bass_kernel_spmd as _run

    nc = _bacc.Bacc("TRN2", target_bir_lowering=False, num_devices=1)
    arrays, aps = {}, {}
    for name in _INS:
        arr = _np.ascontiguousarray(inputs[name])
        arrays["in_" + name] = arr
        aps[name] = nc.dram_tensor("in_" + name, arr.shape, _mybir.dt.from_np(arr.dtype), kind="ExternalInput").ap()
    out = nc.dram_tensor("out", inputs["x"].shape, _mybir.dt.float32, kind="ExternalOutput").ap()
    build_program(nc, aps, out)
    r = _run(nc, [arrays], core_ids=[0])
    return r.results[0]["out"]
```

```python
from contextlib import ExitStack

import concourse.bass as bass
from concourse import mybir

F32 = mybir.dt.float32
F32R = mybir.dt.float32r
ALU = mybir.AluOpType
ACT = mybir.ActivationFunctionType
AX_X = mybir.AxisListType.X

P = 128
EPS = 1e-5
HEADS = 8
BIG = 3.0e38


def wait_apart(eng, begun, sem, value):
    value = value if isinstance(value, int) else eng.to_reg(value)
    eng.wait_ge(begun, 1)
    eng.wait_ge(sem, value)


def make_identity(nc, pool, ident, made):
    nc.gpsimd.memset(ident[:], 0.0).then_inc(made, 1)
    pool.wait_ge(made, 1)
    nc.gpsimd.affine_select(out=ident[:], in_=ident[:], compare_op=ALU.not_equal, fill=1.0, base=0,
                            pattern=[[-1, P]], channel_multiplier=1).then_inc(made, 1)


def graph_phase(nc, a, x_mid, mask, shared):
    B, N, D = a["x"].shape
    NT, DC = N // P, D // P
    HALF = N // 2
    HT = HALF // P
    SLOTS = 4
    ROUNDS = B // SLOTS
    YG = 2 * DC
    with ExitStack() as ctx:
        def sb(name, shape, dt=F32):
            return ctx.enter_context(nc.sbuf_tensor("g_" + name, shape, dt))

        def sem(name):
            return ctx.enter_context(nc.semaphore("g_" + name))

        ident = sb("ident", [P, P])
        adjT_hi = sb("adjT_hi", [P, NT, N], F32R)
        adjT_lo = sb("adjT_lo", [P, NT, N], F32R)
        x_sb = shared + [sb(f"x{i}", [P, NT, D]) for i in range(2, SLOTS)]
        hn = sb("hn", [P, NT, D])
        h_hi = [sb(f"h_hi{i}", [P, NT, D], F32R) for i in range(2)]
        h_lo = [sb(f"h_lo{i}", [P, NT, D], F32R) for i in range(2)]
        yT_hi = sb("yT_hi", [P, DC, N], F32R)
        yT_lo = sb("yT_lo", [P, DC, N], F32R)
        w_raw = sb("w_raw", [P, 2, DC, D])
        w_hi = sb("w_hi", [P, 2, DC, D], F32R)
        w_lo = sb("w_lo", [P, 2, DC, D], F32R)
        bias = sb("bias", [P, 2, D])
        stats = sb("stats", [P, NT, 6])
        mv = sb("mv", [P, NT, 2])
        var_eps = sb("var_eps", [P, NT])
        rstd = sb("rstd", [P, NT])
        half_neg = sb("half_neg", [P, NT])
        next_stats = sb("next_stats", [P, NT, 6])
        next_mv = sb("next_mv", [P, NT, 2])
        next_rstd = sb("next_rstd", [P, NT])
        adj_copy = sb("adj_copy", [P, N])
        deg = sb("deg", [P, NT])
        deg_pos = sb("deg_pos", [P, NT])
        deg_floor = sb("deg_floor", [P, NT])
        deg_is = sb("deg_is", [P, NT])
        spare = sb("spare", [P, NT])
        ps = [ctx.enter_context(nc.psum_tensor(f"g_ps{i}", [P, 512], F32)) for i in range(8)]
        y_ps, w_ps = ps[:4], ps[4:]

        made = sem("made")
        adj_in = [sem(f"adj_in{i}") for i in range(2)]
        w_in = sem("w_in")
        x_in = [sem(f"x_in{i}") for i in range(SLOTS)]
        x_stored = [sem(f"x_stored{i}") for i in range(SLOTS)]
        at_mm = sem("at_mm")
        at_hi = sem("at_hi")
        at_free = sem("at_free")
        w_hi_done = sem("w_hi_done")
        w_split = sem("w_split")
        deg_done = sem("deg_done")
        r_chain = sem("r_chain")
        stat_done = sem("stat_done")
        mv_done = sem("mv_done")
        ln_chain = sem("ln_chain")
        hn_done = sem("hn_done")
        xb_done = sem("xb_done")
        relu_hi = sem("relu_hi")
        h_done = sem("h_done")
        y_mm = sem("y_mm")
        y_hi_done = sem("y_hi_done")
        y_free = sem("y_free")
        w_mm = sem("w_mm")
        w_free = sem("w_free")
        mask_done = sem("mask_done")
        next_in = sem("next_in")
        raw_in = sem("raw_in")
        next_stat = sem("next_stat")
        next_mean = sem("next_mean")
        next_chain = sem("next_chain")
        next_done = sem("next_done")
        block = ctx.enter_context(nc.Block())

        AT = 2 * NT

        def job_of(m):
            return m % 4 // 2, 2 * (m // 4) + m % 2, m % 2

        def x_rows(dram, batch):
            return dram[batch].rearrange("(t p) d -> p t d", p=P)

        @block.sync
        def _(sp):
            sp.dma_start(x_sb[0][:], x_rows(a["x"], 0)).then_inc(x_in[0], 16)
            for t in range(NT):
                sp.dma_start(mask[:, t, :], a["adj"][t * P:(t + 1) * P, :]).then_inc(adj_in[t // HT], 16)
            for layer, name in enumerate(("L0_gnn", "L1_gnn")):
                sp.dma_start(w_raw[:, layer], a[name + "_weight"].rearrange("(c p) o -> p c o", p=P)).then_inc(w_in, 16)
                sp.dma_start(bias[:, layer], a[name + "_bias"].partition_broadcast(P)).then_inc(w_in, 16)
            for s in range(1, SLOTS):
                sp.dma_start(x_sb[s][:], x_rows(a["x"], s)).then_inc(x_in[s], 16)
            raw = shared[1][:].rearrange("p t d -> p (t d)").rearrange("p (c o) -> p c o", c=DC)
            for rnd in range(ROUNDS):
                for s in range(SLOTS):
                    job = 8 * rnd + 4 * (s // 2) + 2 + s % 2
                    sp.wait_ge(w_free, 4 * (job + 2))
                    sp.dma_start(x_rows(x_mid, SLOTS * rnd + s), x_sb[s][:]).then_inc(x_stored[s], 16)
                    if rnd + 1 < ROUNDS:
                        sp.wait_ge(x_stored[s], 16 * (rnd + 1))
                        sp.dma_start(x_sb[s][:], x_rows(a["x"], SLOTS * (rnd + 1) + s)).then_inc(x_in[s], 16)
                    elif s < 2:
                        sp.wait_ge(x_stored[s], 16 * ROUNDS)
                        if s == 0:
                            sp.dma_start(shared[0][:], x_rows(x_mid, 0)).then_inc(next_in, 16)
                        else:
                            sp.dma_start(raw[:, :, 0:3 * D], a["L2_gnn_w_qkv"].rearrange("(c p) o -> p c o", p=P)).then_inc(raw_in, 16)
                            sp.dma_start(raw[:, :, 3 * D:], a["L2_gnn_w_proj"].rearrange("(c p) o -> p c o", p=P)).then_inc(raw_in, 16)
            for s in range(2, SLOTS):
                sp.wait_ge(x_stored[s], 16 * ROUNDS)
            sp.wait_ge(raw_in, 32)

        @block.tensor
        def _(pe):
            mm = nc.tensor.matmul
            pe.wait_ge(made, 2)
            for n in range(AT):
                m, nh = n % NT, n // NT
                pe.wait_ge(adj_in[nh], 16 * HT)
                if n >= 8:
                    pe.wait_ge(at_free, n - 7)
                for i in range(HT):
                    last = nc.tensor.transpose(ps[n % 8][:, i * P:(i + 1) * P],
                                               mask[:, nh * HT + i, m * P:(m + 1) * P], ident[:])
                last.then_inc(at_mm, 1)

            def split_product(out, stat, mov, first, final):
                (s_hi, s_lo), (m_hi, m_lo) = stat, mov
                mm(out, s_hi, m_hi, start=first, stop=False)
                mm(out, s_hi, m_lo, start=False, stop=False)
                return mm(out, s_lo, m_hi, start=False, stop=final)

            def y_group(job, g, s):
                nh, c = g // DC, g % DC
                pe.wait_ge(y_free, 4 * job + g + 1)
                for m in range(NT):
                    stat = (h_hi[s][:, m, c * P:(c + 1) * P], h_lo[s][:, m, c * P:(c + 1) * P])
                    mov = (adjT_hi[:, m, nh * HALF:(nh + 1) * HALF], adjT_lo[:, m, nh * HALF:(nh + 1) * HALF])
                    last = split_product(y_ps[g][:], stat, mov, m == 0, m == NT - 1)
                last.then_inc(y_mm, 1)

            def w_blocks(job, layer, qs):
                for q in qs:
                    pe.wait_ge(y_free, 4 * job + DC * (q // 2 + 1) + 4)
                    pe.wait_ge(w_free, 4 * job + q + 1)
                    for i in range(2):
                        t = 2 * q + i
                        for c in range(DC):
                            stat = (yT_hi[:, c, t * P:(t + 1) * P], yT_lo[:, c, t * P:(t + 1) * P])
                            mov = (w_hi[:, layer, c, :], w_lo[:, layer, c, :])
                            last = split_product(w_ps[q][:, i * D:(i + 1) * D], stat, mov, c == 0, c == DC - 1)
                    last.then_inc(w_mm, 1)

            pe.wait_ge(at_free, AT)
            pe.wait_ge(w_split, 1)
            with pe.Fori(0, ROUNDS) as rnd:
                for m in range(8):
                    job = 8 * rnd + m
                    layer, _, s = job_of(m)
                    pe.wait_ge(h_done, job + 1)
                    y_group(job, 0, s)
                    if m > 0:
                        w_blocks(job - 1, job_of(m - 1)[0], (2, 3))
                    y_group(job, 1, s)
                    y_group(job, 2, s)
                    w_blocks(job, layer, (0, 1))
                    y_group(job, 3, s)
                w_blocks(8 * rnd + 7, 1, (2, 3))

        @block.scalar
        def _(act):
            for n in range(AT):
                m, nh = n % NT, n // NT
                act.wait_ge(at_mm, n + 1)
                nc.scalar.activation(adjT_hi[:, m, nh * HALF:(nh + 1) * HALF], ps[n % 8][:], ACT.Copy).then_inc(at_hi, 1)
            act.wait_ge(w_in, 64)
            nc.scalar.activation(w_hi[:], w_raw[:], ACT.Copy).then_inc(w_hi_done, 1)
            for t in range(NT):
                if t:
                    act.wait_ge(deg_done, t)
                nc.scalar.activation(adj_copy[:], mask[:, t, :], ACT.Copy, accum_out=deg[:, t:t + 1]).then_inc(deg_done, 1)
            with act.Fori(0, 8 * ROUNDS) as job:
                for g in range(YG):
                    nh, c = g // DC, g % DC
                    act.wait_ge(y_mm, 4 * job + g + 1)
                    nc.scalar.activation(yT_hi[:, c, nh * HALF:(nh + 1) * HALF], y_ps[g][:], ACT.Copy).then_inc(y_hi_done, 1)

        @block.gpsimd
        def _(pool):
            make_identity(nc, pool, ident, made)
            nc.gpsimd.memset(half_neg[:], -0.5).then_inc(made, 1)
            pool.wait_ge(made, 3)
            chain = 0
            for job in range(8 * ROUNDS):
                layer, s, _ = job_of(job % 8)
                pool.wait_ge(mv_done, job + 1)
                nc.gpsimd.tensor_scalar(var_eps[:], mv[:, :, 1], EPS, None, ALU.add).then_inc(ln_chain, 1)
                pool.wait_ge(ln_chain, chain + 1)
                nc.gpsimd.tensor_tensor(rstd[:], var_eps[:], half_neg[:], op=ALU.pow).then_inc(ln_chain, 1)
                if layer:
                    pool.wait_ge(ln_chain, chain + 2)
                    nc.gpsimd.tensor_tensor(rstd[:], rstd[:], deg_is[:], op=ALU.mult).then_inc(ln_chain, 1)
                chain += 2 + layer
                if job == 1:
                    pool.wait_ge(deg_done, NT)
                    nc.gpsimd.tensor_scalar(deg_floor[:], deg[:], 1e-30, None, ALU.max).then_inc(r_chain, 1)
                    nc.gpsimd.tensor_scalar(deg_pos[:], deg[:], 0.0, None, ALU.is_gt).then_inc(r_chain, 1)
                    pool.wait_ge(r_chain, 2)
                    nc.gpsimd.tensor_tensor(deg_is[:], deg_floor[:], half_neg[:], op=ALU.pow).then_inc(r_chain, 1)
                    pool.wait_ge(r_chain, 3)
                    nc.gpsimd.tensor_tensor(deg_is[:], deg_is[:], deg_pos[:], op=ALU.mult).then_inc(r_chain, 1)
                    pool.wait_ge(r_chain, 4)
                pool.wait_ge(hn_done, job + 1)
                if job == 0:
                    pool.wait_ge(w_in, 64)
                nc.gpsimd.tensor_tensor(x_sb[s][:], x_sb[s][:],
                                        bias[:, layer:layer + 1, :].to_broadcast([P, NT, D]), op=ALU.add).then_inc(xb_done, 1)
            pool.wait_ge(next_mean, 1)
            nc.gpsimd.tensor_scalar(next_rstd[:], next_mv[:, :, 1], EPS, None, ALU.add).then_inc(next_chain, 1)
            pool.wait_ge(next_chain, 1)
            nc.gpsimd.tensor_tensor(next_rstd[:], next_rstd[:], half_neg[:], op=ALU.pow).then_inc(next_chain, 1)

        @block.vector
        def _(dve):
            def rstd_steps(job):
                return 2 * (job + 1) + 2 * (job // 4) + max(0, job % 4 - 1)

            def ln_stats(job):
                layer, s, _ = job_of(job % 8)
                if layer == 0:
                    dve.wait_ge(x_in[s], 16 * (job // 8 + 1))
                else:
                    dve.wait_ge(w_free, 4 * job)
                for t in range(NT):
                    nc.vector.bn_stats(stats[:, t, :], x_sb[s][:, t, :]).then_inc(stat_done, 1)
                dve.wait_ge(stat_done, 8 * job + 8)
                for t in range(NT):
                    last = nc.vector.bn_aggr(mv[:, t, :], stats[:, t, :])
                last.then_inc(mv_done, 1)

            def norm_split(job):
                _, s, b = job_of(job % 8)
                dve.wait_ge(ln_chain, rstd_steps(job))
                for t in range(NT):
                    last = nc.vector.tensor_scalar(hn[:, t, :], x_sb[s][:, t, :], mv[:, t, 0:1], rstd[:, t:t + 1],
                                                   ALU.subtract, ALU.mult)
                last.then_inc(hn_done, 1)
                dve.wait_ge(hn_done, job + 1)
                for th in range(2):
                    part = slice(th * HT, (th + 1) * HT)
                    nc.vector.tensor_scalar(h_hi[b][:, part, :], hn[:, part, :], 0.0, None, ALU.max).then_inc(relu_hi, 1)
                for th in range(2):
                    part = slice(th * HT, (th + 1) * HT)
                    dve.wait_ge(relu_hi, 2 * job + th + 1)
                    last = nc.vector.scalar_tensor_tensor(
                        out=h_lo[b][:, part, :], in0=hn[:, part, :], scalar=0.0,
                        in1=h_hi[b][:, part, :].bitcast(F32), op0=ALU.max, op1=ALU.subtract)
                last.then_inc(h_done, 1)

            def y_lo(job, g):
                nh, c = g // DC, g % DC
                dve.wait_ge(y_hi_done, 4 * job + g + 1)
                cols = slice(nh * HALF, (nh + 1) * HALF)
                nc.vector.tensor_tensor(yT_lo[:, c, cols], y_ps[g][:], yT_hi[:, c, cols].bitcast(F32),
                                        op=ALU.subtract).then_inc(y_free, 1)

            def add_out(job, qs):
                layer, s, _ = job_of(job % 8)
                dve.wait_ge(xb_done, job + 1)
                for q in qs:
                    dve.wait_ge(w_mm, 4 * job + q + 1)
                    for i in range(2):
                        t = 2 * q + i
                        last = nc.vector.scalar_tensor_tensor(
                            out=x_sb[s][:, t, :], in0=w_ps[q][:, i * D:(i + 1) * D],
                            scalar=deg_is[:, t:t + 1] if layer else 1.0, in1=x_sb[s][:, t, :],
                            op0=ALU.mult, op1=ALU.add)
                    last.then_inc(w_free, 1)

            ln_stats(0)
            norm_split(0)
            for n in range(AT):
                m, nh = n % NT, n // NT
                dve.wait_ge(at_hi, n + 1)
                cols = slice(nh * HALF, (nh + 1) * HALF)
                nc.vector.tensor_tensor(adjT_lo[:, m, cols], ps[n % 8][:], adjT_hi[:, m, cols].bitcast(F32),
                                        op=ALU.subtract).then_inc(at_free, 1)
            dve.wait_ge(w_hi_done, 1)
            nc.vector.tensor_tensor(w_lo[:], w_raw[:], w_hi[:].bitcast(F32), op=ALU.subtract).then_inc(w_split, 1)
            for t in range(NT):
                nc.vector.memset(spare[:, t:t + 1], 0.0).then_inc(y_free if t < 4 else w_free, 1)
            jobs = 8 * ROUNDS
            for job in range(jobs):
                if job % 8:
                    add_out(job - 1, (2, 3))
                y_lo(job, 0)
                if job + 1 < jobs:
                    ln_stats(job + 1)
                y_lo(job, 1)
                if job + 1 < jobs:
                    norm_split(job + 1)
                if job == jobs - 2:
                    dve.wait_ge(next_in, 16)
                    for t in range(NT):
                        nc.vector.bn_stats(next_stats[:, t, :], shared[0][:, t, :]).then_inc(next_stat, 1)
                    dve.wait_ge(next_stat, NT)
                    for t in range(NT):
                        last = nc.vector.bn_aggr(next_mv[:, t, :], next_stats[:, t, :])
                    last.then_inc(next_mean, 1)
                if job == jobs - 1:
                    dve.wait_ge(next_chain, 2)
                    for t in range(NT):
                        nc.vector.tensor_scalar(shared[0][:, t, :], shared[0][:, t, :], next_mv[:, t, 0:1],
                                                next_rstd[:, t:t + 1], ALU.subtract, ALU.mult).then_inc(next_done, 1)
                y_lo(job, 2)
                add_out(job, (0, 1))
                y_lo(job, 3)
                if job % 8 == 7:
                    add_out(job, (2, 3))
                if job == 1:
                    dve.wait_ge(deg_done, NT)
                    for t in range(NT):
                        nc.vector.tensor_scalar(mask[:, t, :], mask[:, t, :], 0.0, BIG, ALU.is_equal, ALU.mult).then_inc(mask_done, 1)
            dve.wait_ge(mask_done, NT)
            dve.wait_ge(next_done, NT)


UNITS = 64
EARLY = [(9, ("norm", 3)), (11, ("turn", 0)), (13, ("out", 0)), (15, ("turn", 1)), (17, ("out", 1)),
         (26, ("turn", 2)), (28, ("out", 2)), (30, ("turn", 3)), (32, ("out", 3))]
MID = [(18, ("qk", 1, 0, 0)), (20, ("qk", 1, 1, 0)), (22, ("qk", 1, 0, 1)), (24, ("qk", 1, 1, 1)),
       (33, ("norm", 0)), (49, ("norm", 1)), (60, ("norm", 2))]
NEXT = [(35, ("h", 0, 0)), (37, ("h", 0, 1)), (40, ("h", 1, 0)), (42, ("h", 1, 1)),
        (44, ("v", 0)), (45, ("v", 1)), (47, ("v", 2)), (48, ("v", 3)),
        (51, ("qk", 0, 0, 0)), (53, ("qk", 0, 1, 0)), (54, ("qk", 0, 0, 1)), (56, ("qk", 0, 1, 1))]
FIRST = [("h", 0, 0), ("h", 0, 1), ("h", 1, 0), ("h", 1, 1),
         ("qk", 0, 0, 0), ("qk", 0, 1, 0), ("qk", 0, 0, 1), ("qk", 0, 1, 1), ("v", 0), ("v", 1), ("v", 2), ("v", 3)]
LAST = [("norm", 3), ("turn", 0), ("turn", 1), ("out", 0), ("turn", 2), ("out", 1), ("turn", 3), ("out", 2), ("out", 3)]
FIRST_QK = 8
SHORT = ("h", "turn")
LN_STEP = 16
PER_JOB = len(EARLY) + len(MID) + len(NEXT)


def blocks_of(first, more):
    table = sorted((EARLY if not first else []) + MID + (NEXT if more else []))
    skip = len(EARLY) if first else 0
    return {step: (skip + i, what) for i, (step, what) in enumerate(table)}


def scalar_halves(table):
    return {u for u in range(UNITS)
            if (table[u][1][0] in ("v", "norm", "out") if u in table else u % 4 == 3 and u % 16 != 7)}


def attention_phase(nc, a, x_mid, x_mid2, out, mask, shared):
    B, N, D = a["x"].shape
    NT, DC = N // P, D // P
    HD = D // HEADS
    HALF = N // 2
    HT = HALF // P
    JOBS = 2 * B
    SCALE = float(HD) ** -0.5
    GH = P // HD
    RING = 4
    XE = 3
    with ExitStack() as ctx:
        def sb(name, shape, dt=F32):
            return ctx.enter_context(nc.sbuf_tensor("t_" + name, shape, dt))

        def sem(name):
            return ctx.enter_context(nc.semaphore("t_" + name))

        def pb(name, width):
            return ctx.enter_context(nc.psum_tensor("t_" + name, [P, width], F32))

        ident = sb("ident", [P, P])
        w_hi = [sb(f"w_hi{i}", [P, DC, 4 * D], F32R) for i in range(2)]
        w_lo = [sb(f"w_lo{i}", [P, DC, 4 * D], F32R) for i in range(2)]
        b_qk = sb("b_qk", [P, 2, 2, 2])
        b_v = sb("b_v", [P, 1, D])
        b_out = [sb(f"b_out{i}", [P, 1, D]) for i in range(2)]
        gamma = sb("gamma", [P, 1, D])
        beta = sb("beta", [P, 1, D])
        xa, v_sb = shared
        hT_hi = sb("hT_hi", [P, DC, N], F32R)
        hT_lo = sb("hT_lo", [P, DC, N], F32R)
        st_hi = [sb(f"st_hi{i}", [P, N], F32R) for i in range(2)]
        st_lo = [sb(f"st_lo{i}", [P, N], F32R) for i in range(2)]
        q4 = [sb(f"q4_{i}", [P, N], F32R) for i in range(2)]
        k4 = [sb(f"k4_{i}", [P, N], F32R) for i in range(2)]
        T = [sb(f"T{i}", [P, N]) for i in range(RING)]
        PT = sb("PT", [P, NT, NT, P])
        low = sb("low", [P, RING])
        rsum = sb("rsum", [P, UNITS])
        rinv = sb("rinv", [P, UNITS])
        ot_sb = sb("ot", [P, 512])
        o_sb = sb("o", [P, NT, D])
        oT_hi = sb("oT_hi", [P, 512], F32R)
        oT_lo = sb("oT_lo", [P, 512], F32R)
        xe = [sb(f"xe{i}", [P, 2, D]) for i in range(XE)]
        proj = [sb(f"proj{i}", [P, 2, D]) for i in range(2)]
        stats = sb("stats", [P, NT, 6])
        mv = sb("mv", [P, NT, 2])
        var_eps = sb("var_eps", [P, NT])
        rstd = sb("rstd", [P, NT])
        half_neg = sb("half_neg", [P, NT])
        stats2 = [sb(f"stats2_{i}", [P, 2, 6]) for i in range(2)]
        mv2 = [sb(f"mv2_{i}", [P, 2, 2]) for i in range(2)]
        var2 = sb("var2", [P, 2])
        rstd2 = [sb(f"rstd2_{i}", [P, 2]) for i in range(2)]
        spare = sb("spare", [P, 4])

        s_ps = [pb(f"s_ps{i}", N) for i in range(2)]
        pt_ps = [pb(f"pt_ps{i}", 512) for i in range(2)]
        ot_ps = pb("ot_ps", 512)
        g_ps = pb("g_ps", 512)

        made = sem("made")
        raw_in = sem("raw_in")
        bias_in = sem("bias_in")
        bias_zero = sem("bias_zero")
        bias_done = sem("bias_done")
        w_hi_done = sem("w_hi_done")
        w_split = sem("w_split")
        xa_in = sem("xa_in")
        stat_done = sem("stat_done")
        mv_done = sem("mv_done")
        ln_chain = sem("ln_chain")
        hn_done = sem("hn_done")
        g_mm = sem("g_mm")
        g_free = sem("g_free")
        h_hi_done = sem("h_hi_done")
        qk_hi_done = sem("qk_hi_done")
        oT_hi_done = sem("oT_hi_done")
        head_in = [sem(f"head_in{i}") for i in range(2)]
        s_done = sem("s_done")
        t_done = sem("t_done")
        p_done = sem("p_done")
        tr_done = [sem(f"tr_done{i}") for i in range(2)]
        pt_done = [sem(f"pt_done{i}") for i in range(2)]
        av_done = sem("av_done")
        ot_done = sem("ot_done")
        rinv_done = sem("rinv_done")
        xe_in = [sem(f"xe_in{i}") for i in range(4)]
        v_moved = sem("v_moved")
        xe_biased = sem("xe_biased")
        x_stored = sem("x_stored")
        stat2_done = sem("stat2_done")
        mv2_done = sem("mv2_done")
        var2_done = sem("var2_done")
        rstd2_done = sem("rstd2_done")
        proj_added = sem("proj_added")
        centered = sem("centered")
        ln2_chain = sem("ln2_chain")
        epi_done = sem("epi_done")
        mask_in = [sem(f"mask_in{t}") for t in range(NT)]
        mask3_done = sem("mask3_done")
        block = ctx.enter_context(nc.Block())

        FIRST_BLOCKS = len(FIRST)

        def block_at(job, k):
            return PER_JOB * job + FIRST_BLOCKS - len(EARLY) + k

        def jobs(eng, body):
            body(0, 0, None, 0)
            with eng.Fori(1, B - 1) as job:
                body(job, 0, 0, 0)
            body(B - 1, 0, 0, 1)
            body(B, 1, 0, 1)
            with eng.Fori(B + 1, JOBS - 1) as job:
                body(job, 1, 1, 1)
            body(JOBS - 1, 1, 1, None)

        def tail_block(k):
            return block_at(JOBS, k) - len(NEXT)

        banks = [g_ps, pt_ps[0], pt_ps[1], ot_ps]

        def bank(k):
            return banks[0 if k is None else k % 4]

        def oT(p, last):
            return (st_hi[0][:, 0:512], st_lo[0][:, 0:512]) if last and p % 2 else (oT_hi[:], oT_lo[:])

        def res_of(job, p):
            return proj[0] if p == XE and isinstance(job, int) and job == JOBS - 1 else xe[p % XE]

        def raw_weights(layer):
            flat = PT[:].rearrange("p a b c -> p (a b c)") if layer else v_sb[:].rearrange("p t d -> p (t d)")
            return flat[:, 0:DC * 4 * D].rearrange("p (c o) -> p c o", c=DC)

        def pt_of(u, half):
            qt, keys = u % NT, slice(half * HT, (half + 1) * HT)
            return PT[:, qt, keys, :] if u // NT % 2 == 0 else PT[:, keys, qt, :]

        def x_of(layer, batch):
            return (x_mid, x_mid2)[layer][batch]

        @block.sync
        def _(sp):
            for i, name in enumerate(("Wq", "Wk", "Wv", "Wo")):
                sp.dma_start(raw_weights(1)[:, :, i * D:(i + 1) * D],
                             a["L3_gnn_" + name].rearrange("(c p) o -> p c o", p=P)).then_inc(raw_in, 16)
            for dst, name in ((b_v, "L3_gnn_bv"), (b_out[0], "L2_gnn_b_proj"), (b_out[1], "L3_gnn_bo"),
                              (gamma, "L2_gnn_ln_gamma"), (beta, "L2_gnn_ln_beta")):
                sp.dma_start(dst[:, 0, :], a[name].partition_broadcast(P)).then_inc(bias_in, 16)
            for w, name in enumerate(("L3_gnn_bq", "L3_gnn_bk")):
                for g in range(2):
                    sp.dma_start(b_qk[:, 1, w, g:g + 1], a[name][g * P:(g + 1) * P].rearrange("(p o) -> p o", o=1)).then_inc(bias_in, 16)

            def load_head(job, h, slot_free, staged):
                s, rows = h % 2, slice((h % GH) * HD, (h % GH + 1) * HD)
                if slot_free is not None:
                    wait_apart(sp, raw_in, s_done, slot_free)
                if staged is not None:
                    sp.wait_ge(g_free, staged)
                for part in range(4):
                    dst = slice(part * HD, (part + 1) * HD)
                    sp.dma_start(q4[s][dst, :].bitcast(F32), (st_hi, st_lo)[part // 2][0][rows, :].bitcast(F32)).then_inc(head_in[s], 16)
                    sp.dma_start(k4[s][dst, :].bitcast(F32), (st_hi, st_lo)[part % 2][1][rows, :].bitcast(F32)).then_inc(head_in[s], 16)

            def load_xe(job, layer, p):
                batch = job - B * layer
                sp.dma_start(res_of(job, p)[:], x_of(layer, batch)[2 * p * P:2 * (p + 1) * P, :]
                             .rearrange("(t p) d -> p t d", p=P)).then_inc(xe_in[p], 16)

            def store(job, layer, p, n):
                batch = job - B * layer
                if layer == 0:
                    wait_apart(sp, raw_in, epi_done, 4 * job + p + 3)
                else:
                    wait_apart(sp, raw_in, g_free, n + 1)
                sp.dma_start((x_mid2, out)[layer][batch, 2 * p * P:2 * (p + 1) * P, :]
                             .rearrange("(t p) d -> p t d", p=P), res_of(job, p)[:]).then_inc(x_stored, 16)

            def after_store(job, p):
                wait_apart(sp, raw_in, x_stored, 16 * (4 * job + p + 1))

            def body(job, layer, before, after):
                table = blocks_of(before is None, after is not None)
                at = {what: block_at(job, k) for k, what in table.values()}
                if before is not None:
                    for p in range(XE):
                        load_xe(job - 1, before, p)
                if after is not None:
                    wait_apart(sp, raw_in, v_moved, job + 1)
                    sp.dma_start(xa[:], x_of(after, job + 1 - B * after).rearrange("(t p) d -> p t d", p=P)).then_inc(xa_in, 16)
                load_head(job, 2, UNITS * job + 8, None)
                load_head(job, 3, UNITS * job + 16, None)
                if before is not None:
                    store(job - 1, before, 0, at[("out", 0)])
                    after_store(job - 1, 0)
                    load_xe(job - 1, before, 3)
                    store(job - 1, before, 1, at[("out", 1)])
                load_head(job, 4, UNITS * job + 24, at[("qk", 1, 1, 1)] + 1)
                if before is not None:
                    store(job - 1, before, 2, at[("out", 2)])
                load_head(job, 5, UNITS * job + 32, None)
                if before is not None:
                    store(job - 1, before, 3, at[("out", 3)])
                load_head(job, 6, UNITS * job + 40, None)
                load_head(job, 7, UNITS * job + 48, None)
                if before is not None:
                    after_store(job - 1, 3)
                if after is not None:
                    load_head(job + 1, 0, UNITS * job + 56, at[("qk", 0, 1, 1)] + 1)
                    load_head(job + 1, 1, UNITS * job + 64, None)

            load_head(0, 0, None, FIRST_QK)
            load_head(0, 1, None, None)
            jobs(sp, body)
            for p in range(4):
                load_xe(JOBS - 1, 1, p)
            for p in range(4):
                store(JOBS - 1, 1, p, tail_block(LAST.index(("out", p))))
            after_store(JOBS - 1, 3)

        @block.tensor
        def _(pe):
            mm = nc.tensor.matmul

            def split_product(dst, stat, mov, first, final):
                (s_hi, s_lo), (m_hi, m_lo) = stat, mov
                mm(dst, s_hi, m_hi, start=first, stop=False)
                mm(dst, s_hi, m_lo, start=False, stop=False)
                return mm(dst, s_lo, m_hi, start=False, stop=final)

            def scores(job, u, wait):
                job, u = (job + 1, u - UNITS) if u >= UNITS else (job, u)
                h, qt = u // NT, u % NT
                if qt == 0:
                    pe.wait_ge(head_in[h % 2], 128 * (4 * job + h // 2 + 1))
                if wait is not None:
                    pe.wait_ge(t_done, wait)
                for half in range(2):
                    cols = slice(half * HALF, (half + 1) * HALF)
                    last = mm(s_ps[u % 2][:, cols], q4[h % 2][:, qt * P:(qt + 1) * P], k4[h % 2][:, cols],
                              start=True, stop=True)
                last.then_inc(s_done, 1)

            def transposes(job, u):
                pe.wait_ge(p_done, UNITS * job + u + 1)
                for half in range(2):
                    pe.wait_ge(pt_done[half], UNITS * job + u + 1)
                    for i in range(HT):
                        kt = half * HT + i
                        last = nc.tensor.transpose(pt_ps[half][:, i * P:(i + 1) * P],
                                                   T[u % RING][:, kt * P:(kt + 1) * P], ident[:])
                    last.then_inc(tr_done[half], 1)

            def values(job, u):
                h, kt = u // NT - 1 if u >= NT else HEADS - 1, u % NT
                if kt % HT == 0:
                    pe.wait_ge(pt_done[kt // HT], UNITS * job + u - kt + 1)
                if kt == 0 and h == HEADS // 2:
                    pe.wait_ge(v_moved, job + 1)
                if kt == 0 and h % 2 == 0 and not (isinstance(job, int) and job == 0 and h == 0):
                    pe.wait_ge(ot_done, 4 * job + h // 2)
                for j in range(HT):
                    probs = PT[:, j:NT:HT, kt, :] if h % 2 == 0 else PT[:, kt, j:NT:HT, :]
                    last = mm(ot_ps[j * HD:(j + 1) * HD, h % 2 * 2 * P:(h % 2 + 1) * 2 * P],
                              v_sb[:, kt, h * HD:(h + 1) * HD], probs, start=kt == 0, stop=kt == NT - 1)
                last.then_inc(av_done, 1)

            def one_block(n, what, layer, job_of_h, k=None, last=False):
                ps = bank(k)
                if k is None:
                    pe.wait_ge(g_free, n)
                else:
                    needs = {"h": 0, "qk": 4, "v": 4, "norm": 0, "turn": 1, "out": 0}[what[0]]
                    if what[0] == "out":
                        needs = LAST.index(("turn", what[1])) + 1
                    free = n - k + max(needs, k - 3)
                    if free:
                        pe.wait_ge(g_free, free)
                kind = what[0]
                if kind == "norm":
                    for i in range(4):
                        final = nc.tensor.transpose(ps[:, i * P:(i + 1) * P], ot_sb[:, i * P:(i + 1) * P], ident[:])
                elif kind == "turn":
                    for i in range(4):
                        t, c = 2 * what[1] + i // DC, i % DC
                        final = nc.tensor.transpose(ps[:, i * P:(i + 1) * P], o_sb[:, t, c * P:(c + 1) * P], ident[:])
                elif kind == "out":
                    hi, lo = oT(what[1], last)
                    for i in range(2):
                        for c in range(DC):
                            at = slice((DC * i + c) * P, (DC * i + c + 1) * P)
                            cols = slice(3 * D, 4 * D)
                            final = split_product(ps[:, i * D:(i + 1) * D], (hi[:, at], lo[:, at]),
                                                 (w_hi[layer][:, c, cols], w_lo[layer][:, c, cols]), c == 0, c == DC - 1)
                elif kind == "h":
                    c, nh = what[1:]
                    if k is None:
                        pe.wait_ge(hn_done, 4 * job_of_h + 2 * nh - 2)
                    for i in range(HT):
                        final = nc.tensor.transpose(ps[:, i * P:(i + 1) * P],
                                                   xa[:, nh * HT + i, c * P:(c + 1) * P], ident[:])
                elif kind == "qk":
                    g, w, nh = what[1:]
                    cols, toks = slice(w * D + g * P, w * D + (g + 1) * P), slice(nh * HALF, (nh + 1) * HALF)
                    for c in range(DC):
                        final = split_product(ps[:], (w_hi[layer][:, c, cols], w_lo[layer][:, c, cols]),
                                             (hT_hi[:, c, toks], hT_lo[:, c, toks]), c == 0, c == DC - 1)
                else:
                    cols = slice(2 * D, 3 * D)
                    for i in range(2):
                        toks = slice((2 * what[1] + i) * P, (2 * what[1] + i + 1) * P)
                        for c in range(DC):
                            final = split_product(ps[:, i * D:(i + 1) * D], (hT_hi[:, c, toks], hT_lo[:, c, toks]),
                                                 (w_hi[layer][:, c, cols], w_lo[layer][:, c, cols]), c == 0, c == DC - 1)
                final.then_inc(g_mm, 1)

            def body(job, layer, before, after):
                table = blocks_of(before is None, after is not None)
                for u in range(UNITS):
                    if u + 2 < UNITS or after is not None:
                        scores(job, u + 2, UNITS * job + u + 1)
                    if u in table:
                        k, what = table[u]
                        lay = before if (u, what) in EARLY else after if (u, what) in NEXT else layer
                        if what[0] == "norm":
                            pe.wait_ge(ot_done, 4 * job + what[1] + 1 if what[1] < 3 else 4 * job)
                        one_block(block_at(job, k), what, lay, job + 1)
                    if u >= NT or before is not None:
                        values(job, u)
                    transposes(job, u)

            pe.wait_ge(made, 3)
            for n, what in enumerate(FIRST):
                if n == 4:
                    pe.wait_ge(w_split, 1)
                one_block(n, what, 0, 0, n)
            scores(0, 0, None)
            scores(0, 1, None)
            pe.wait_ge(w_split, 2)
            jobs(pe, body)
            for u in range(NT):
                values(JOBS, u)
            pe.wait_ge(ot_done, 4 * JOBS)
            for k, what in enumerate(LAST):
                one_block(tail_block(k), what, 1, None, k, True)

        @block.scalar
        def _(act):
            copy = nc.scalar.activation

            def hi_part(n, what, layer, job, k=None, last=False):
                kind, ps = what[0], bank(k)
                if kind == "h":
                    c, nh = what[1:]
                    act.wait_ge(g_mm, n + 1)
                    copy(hT_hi[:, c, nh * HALF:(nh + 1) * HALF], ps[:], ACT.Relu).then_inc(h_hi_done, 1)
                elif kind == "qk":
                    g, w, nh = what[1:]
                    if not (g == 0 and isinstance(job, int) and job == 0):
                        for s in range(2):
                            act.wait_ge(head_in[s], 128 * (4 * job + 2 * g))
                    act.wait_ge(g_mm, n + 1)
                    copy(st_hi[w][:, nh * HALF:(nh + 1) * HALF], ps[:], ACT.Identity,
                         bias=b_qk[:, layer, w, g:g + 1]).then_inc(qk_hi_done, 1)
                elif kind == "turn":
                    act.wait_ge(g_mm, n + 1)
                    copy(oT(what[1], last)[0], ps[:], ACT.Copy).then_inc(oT_hi_done, 1)

            def exp(job, u):
                job, u = (job + 1, u - UNITS) if u >= UNITS else (job, u)
                act.wait_ge(t_done, UNITS * job + u + 1)
                nc.scalar.activation(T[u % RING][:], T[u % RING][:], ACT.Exp, bias=low[:, u % RING:u % RING + 1],
                                     scale=-1.0, accum_out=rsum[:, u:u + 1]).then_inc(p_done, 1)

            def copy_pt(job, u, half):
                act.wait_ge(tr_done[half], UNITS * job + u + 1)
                copy(pt_of(u, half),
                     pt_ps[half][:].rearrange("p (k q) -> p k q", k=HT), ACT.Copy).then_inc(pt_done[half], 1)

            def copy_ot(after):
                act.wait_ge(av_done, after)
                copy(ot_sb[:], ot_ps[:], ACT.Copy).then_inc(ot_done, 1)

            def weights_hi(layer):
                if layer:
                    act.wait_ge(raw_in, 64)
                raw = raw_weights(layer)
                copy(w_hi[layer][:, :, 0:D], raw[:, :, 0:D], ACT.Copy, scale=-SCALE).then_inc(w_hi_done, 1)
                copy(w_hi[layer][:, :, D:], raw[:, :, D:], ACT.Copy).then_inc(w_hi_done, 1)

            weights_hi(0)
            act.wait_ge(bias_zero, 1)
            for n, what in enumerate(FIRST):
                hi_part(n, what, 0, 0, n)
            weights_hi(1)
            act.wait_ge(bias_done, 1)
            exp(0, 0)

            def body(job, layer, before, after):
                table = blocks_of(before is None, after is not None)
                for u in range(UNITS):
                    if u + 1 < UNITS or after is not None:
                        exp(job, u + 1)
                    if u % (2 * NT) == NT - 1 and (u >= NT or before is not None):
                        copy_ot(UNITS * job + u + 1 - NT)
                    halves = (0, 1) if u in scalar_halves(table) else (0,)
                    copy_first = u in table and table[u][1][0] in SHORT
                    if copy_first:
                        for half in halves:
                            copy_pt(job, u, half)
                    if u in table:
                        k, what = table[u]
                        in_next = (u, what) in NEXT
                        hi_part(block_at(job, k), what, after if in_next else layer, job + 1 if in_next else job)
                    if not copy_first:
                        for half in halves:
                            copy_pt(job, u, half)

            jobs(act, body)
            copy_ot(UNITS * JOBS)
            for i in range(2):
                act.wait_ge(head_in[i], 128 * 4 * JOBS)
            for k, what in enumerate(LAST):
                hi_part(tail_block(k), what, 1, None, k, True)

        @block.vector
        def _(dve):
            def masked(job, u, layer):
                job, u = (job + 1, u - UNITS) if u >= UNITS else (job, u)
                qt = u % NT
                if layer == 1 and isinstance(job, int) and job == B:
                    dve.wait_ge(mask3_done, qt + 1)
                wait_apart(dve, made, s_done, UNITS * job + u + 1)
                nc.vector.tensor_tensor_reduce(out=T[u % RING][:], in0=s_ps[u % 2][:], in1=mask[:, qt, :],
                                               scale=1.0, scalar=3.4e38, op0=ALU.add, op1=ALU.min,
                                               accum_out=low[:, u % RING:u % RING + 1]).then_inc(t_done, 1)

            def finish_block(n, what, layer, job, k=None, last=False):
                kind, ps = what[0], bank(k)
                if kind == "h":
                    c, nh = what[1:]
                    cols = slice(nh * HALF, (nh + 1) * HALF)
                    dve.wait_ge(h_hi_done, 4 * job + 2 * c + nh + 1)
                    nc.vector.scalar_tensor_tensor(out=hT_lo[:, c, cols], in0=ps[:], scalar=0.0,
                                                   in1=hT_hi[:, c, cols].bitcast(F32),
                                                   op0=ALU.max, op1=ALU.subtract).then_inc(g_free, 1)
                elif kind == "qk":
                    g, w, nh = what[1:]
                    cols = slice(nh * HALF, (nh + 1) * HALF)
                    dve.wait_ge(qk_hi_done, 8 * job + 4 * g + 2 * nh + w + 1)
                    nc.vector.scalar_tensor_tensor(out=st_lo[w][:, cols], in0=ps[:], scalar=b_qk[:, layer, w, g:g + 1],
                                                   in1=st_hi[w][:, cols].bitcast(F32),
                                                   op0=ALU.add, op1=ALU.subtract).then_inc(g_free, 1)
                elif kind == "v":
                    tiles = slice(2 * what[1], 2 * what[1] + 2)
                    dve.wait_ge(g_mm, n + 1)
                    for g, dst in enumerate((v_sb, xa)):
                        src = ps[:].rearrange("p (t d) -> p t d", t=2)[:, :, g * P:(g + 1) * P]
                        if layer == 0:
                            final = nc.vector.tensor_copy(dst[:, tiles, 0:P], src)
                        else:
                            final = nc.vector.tensor_tensor(dst[:, tiles, 0:P], src,
                                                           b_v[:, :, g * P:(g + 1) * P].to_broadcast([P, 2, P]),
                                                           op=ALU.add)
                    final.then_inc(g_free, 1)
                elif kind == "norm":
                    pr = what[1]
                    cols = slice(16 * pr, 16 * pr + 16)
                    dve.wait_ge(g_mm, n + 1)
                    nc.vector.reciprocal(rinv[:, cols], rsum[:, cols]).then_inc(rinv_done, 1)
                    dve.wait_ge(rinv_done, 4 * job + pr + 1)
                    nc.vector.tensor_tensor(
                        o_sb[:, :, 2 * pr * HD:(2 * pr + 2) * HD].rearrange("p t (h d) -> p h t d", h=2),
                        ps[:].rearrange("p (h t d) -> p h t d", h=2, t=NT),
                        rinv[:, cols].rearrange("p (h t o) -> p h t o", h=2, o=1).to_broadcast([P, 2, NT, HD]),
                        op=ALU.mult).then_inc(g_free, 1)
                elif kind == "turn":
                    dve.wait_ge(oT_hi_done, 4 * job + what[1] + 1)
                    hi, lo = oT(what[1], last)
                    nc.vector.tensor_tensor(lo, ps[:], hi.bitcast(F32), op=ALU.subtract).then_inc(g_free, 1)
                elif layer == 0:
                    p = what[1]
                    b = p % 2
                    dve.wait_ge(epi_done, 4 * job + p + 1)
                    dve.wait_ge(g_mm, n + 1)
                    nc.vector.tensor_tensor(proj[b][:], ps[:].rearrange("p (t d) -> p t d", t=2),
                                            b_out[0][:].to_broadcast([P, 2, D]), op=ALU.add).then_inc(g_free, 1)
                    dve.wait_ge(g_free, n + 1)
                    for i in range(2):
                        nc.vector.bn_stats(stats2[b][:, i, :], proj[b][:, i, :]).then_inc(stat2_done, 1)
                    wait_apart(dve, made, stat2_done, 8 * job + 2 * p + 2)
                    for i in range(2):
                        final = nc.vector.bn_aggr(mv2[b][:, i, :], stats2[b][:, i, :])
                    final.then_inc(mv2_done, 1)
                else:
                    p = what[1]
                    dve.wait_ge(xe_biased, 4 * job + p + 1)
                    dve.wait_ge(g_mm, n + 1)
                    nc.vector.tensor_tensor(res_of(job, p)[:], ps[:].rearrange("p (t d) -> p t d", t=2),
                                            res_of(job, p)[:], op=ALU.add).then_inc(g_free, 1)

            def copy_pt(job, u):
                dve.wait_ge(tr_done[1], UNITS * job + u + 1)
                nc.vector.tensor_copy(pt_of(u, 1),
                                      pt_ps[1][:].rearrange("p (k q) -> p k q", k=HT)).then_inc(pt_done[1], 1)

            def mask3(t):
                dve.wait_ge(mask_in[t], 16)
                nc.vector.tensor_scalar(mask[:, t, :], mask[:, t, :], 1.0, -1.0e9, ALU.subtract, ALU.mult)\
                    .then_inc(mask3_done, 1)

            def ln_stats(job, t):
                if t == 0:
                    dve.wait_ge(xa_in, 16 * job)
                nc.vector.bn_stats(stats[:, t, :], xa[:, t, :]).then_inc(stat_done, 1)

            def ln_mean(job):
                wait_apart(dve, made, stat_done, 8 * job)
                for t in range(NT):
                    last = nc.vector.bn_aggr(mv[:, t, :], stats[:, t, :])
                last.then_inc(mv_done, 1)

            def weights_lo(layer):
                raw = raw_weights(layer)
                dve.wait_ge(w_hi_done, 2 * layer + 2)
                nc.vector.scalar_tensor_tensor(out=w_lo[layer][:, :, 0:D], in0=raw[:, :, 0:D], scalar=-SCALE,
                                               in1=w_hi[layer][:, :, 0:D].bitcast(F32), op0=ALU.mult, op1=ALU.subtract)
                nc.vector.tensor_tensor(w_lo[layer][:, :, D:], raw[:, :, D:], w_hi[layer][:, :, D:].bitcast(F32),
                                        op=ALU.subtract).then_inc(w_split, 1)

            weights_lo(0)
            dve.wait_ge(bias_zero, 1)
            for n, what in enumerate(FIRST):
                finish_block(n, what, 0, 0, n)
            weights_lo(1)
            dve.wait_ge(bias_done, 1)
            masked(0, 0, 0)
            masked(0, 1, 0)
            for half in range(2):
                nc.vector.memset(spare[:, half:half + 1], 0.0).then_inc(pt_done[half], 1)

            def body(job, layer, before, after):
                table = blocks_of(before is None, after is not None)
                for u in range(UNITS):
                    if u + 2 < UNITS or after is not None:
                        masked(job, u + 2, layer if u + 2 < UNITS else after)
                    copy_first = u in table and table[u][1][0] in SHORT
                    if copy_first and u not in scalar_halves(table):
                        copy_pt(job, u)
                    if u in table:
                        k, what = table[u]
                        early, in_next = (u, what) in EARLY, (u, what) in NEXT
                        finish_block(block_at(job, k), what, before if early else after if in_next else layer,
                                     job - 1 if early else job + 1 if in_next else job)
                    if not copy_first and u not in scalar_halves(table):
                        copy_pt(job, u)
                    if after is not None:
                        if LN_STEP <= u < LN_STEP + NT:
                            ln_stats(job + 1, u - LN_STEP)
                        if u == LN_STEP + NT:
                            ln_mean(job + 1)
                    if layer != after and after is not None and u >= UNITS - NT + 1:
                        mask3(u - (UNITS - NT + 1))
                        if u == UNITS - 1:
                            mask3(NT - 1)

            jobs(dve, body)
            for k, what in enumerate(LAST):
                finish_block(tail_block(k), what, 1, JOBS - 1, k, True)

        @block.gpsimd
        def _(pool):
            make_identity(nc, pool, ident, made)
            nc.gpsimd.memset(half_neg[:], -0.5).then_inc(made, 1)
            nc.gpsimd.memset(b_qk[:, 0], 0.0).then_inc(bias_zero, 1)
            pool.wait_ge(bias_in, 144)
            nc.gpsimd.tensor_scalar(b_qk[:, 1, 0, :], b_qk[:, 1, 0, :], -SCALE, None, ALU.mult).then_inc(bias_done, 1)
            pool.wait_ge(made, 3)

            def row_scale(job):
                wait_apart(pool, made, mv_done, job)
                nc.gpsimd.tensor_scalar(var_eps[:], mv[:, :, 1], EPS, None, ALU.add).then_inc(ln_chain, 1)
                pool.wait_ge(ln_chain, 2 * job - 1)
                nc.gpsimd.tensor_tensor(rstd[:], var_eps[:], half_neg[:], op=ALU.pow).then_inc(ln_chain, 1)

            def move_v(job):
                wait_apart(pool, made, g_free, FIRST_BLOCKS if isinstance(job, int) and job == 0 else block_at(job, 0))
                if not (isinstance(job, int) and job == 0):
                    wait_apart(pool, made, av_done, UNITS * job)
                nc.gpsimd.tensor_copy(v_sb[:, :, P:2 * P], xa[:, :, 0:P]).then_inc(v_moved, 1)

            def bias_xe(job, layer, p):
                pool.wait_ge(xe_in[p], 16 * (job + 1))
                nc.gpsimd.tensor_tensor(res_of(job, p)[:], res_of(job, p)[:], (beta, b_out[1])[layer][:].to_broadcast([P, 2, D]),
                                        op=ALU.add).then_inc(xe_biased, 1)

            def add_ln(job, p):
                b = p % 2
                wait_apart(pool, made, mv2_done, 4 * job + p + 1)
                nc.gpsimd.tensor_scalar(var2[:], mv2[b][:, :, 1], EPS, None, ALU.add).then_inc(var2_done, 1)
                pool.wait_ge(xe_biased, 4 * job + p + 1)
                nc.gpsimd.tensor_tensor(res_of(job, p)[:], res_of(job, p)[:], proj[b][:], op=ALU.add).then_inc(proj_added, 1)
                pool.wait_ge(proj_added, 4 * job + p + 1)
                nc.gpsimd.tensor_tensor(proj[b][:], proj[b][:], mv2[b][:, :, 0:1].to_broadcast([P, 2, D]),
                                        op=ALU.subtract).then_inc(ln2_chain, 1)
                pool.wait_ge(var2_done, 4 * job + p + 1)
                nc.gpsimd.tensor_tensor(rstd2[b][:], var2[:], half_neg[:, 0:2], op=ALU.pow).then_inc(rstd2_done, 1)
                pool.wait_ge(ln2_chain, 3 * (4 * job + p) + 1)
                nc.gpsimd.tensor_tensor(proj[b][:], proj[b][:], gamma[:].to_broadcast([P, 2, D]),
                                        op=ALU.mult).then_inc(ln2_chain, 1)
                pool.wait_ge(ln2_chain, 3 * (4 * job + p) + 2)
                pool.wait_ge(rstd2_done, 4 * job + p + 1)
                nc.gpsimd.tensor_tensor(proj[b][:], proj[b][:],
                                        rstd2[b][:].rearrange("p (t o) -> p t o", o=1).to_broadcast([P, 2, D]),
                                        op=ALU.mult).then_inc(ln2_chain, 1)
                pool.wait_ge(ln2_chain, 3 * (4 * job + p) + 3)
                nc.gpsimd.tensor_tensor(res_of(job, p)[:], res_of(job, p)[:], proj[b][:], op=ALU.add).then_inc(epi_done, 1)

            def norm(job):
                pool.wait_ge(ln_chain, 2 * job)
                for p in range(NT // 2):
                    tiles = slice(2 * p, 2 * p + 2)
                    nc.gpsimd.tensor_tensor(xa[:, tiles, :], xa[:, tiles, :], mv[:, tiles, 0:1].to_broadcast([P, 2, D]),
                                            op=ALU.subtract).then_inc(centered, 1)
                    pool.wait_ge(centered, 4 * job + p - 3)
                    nc.gpsimd.tensor_tensor(xa[:, tiles, :], xa[:, tiles, :],
                                            rstd[:, tiles].rearrange("p (t o) -> p t o", o=1).to_broadcast([P, 2, D]),
                                            op=ALU.mult).then_inc(hn_done, 1)

            def load_mask3():
                for t in range(NT):
                    pool.wait_ge(t_done, UNITS * (B - 1) + UNITS - NT + t + 1)
                    pool.dma_start(mask[:, t, :], a["adj"][t * P:(t + 1) * P, :]).then_inc(mask_in[t], 16)

            for b in range(2):
                nc.gpsimd.memset(spare[:, 2 + b:3 + b], 0.0).then_inc(epi_done, 1)

            def body(job, layer, before, after):
                move_v(job)
                if before is not None:
                    for p in range(XE):
                        bias_xe(job - 1, before, p)
                    if before == 0:
                        add_ln(job - 1, 0)
                        add_ln(job - 1, 1)
                    bias_xe(job - 1, before, XE)
                if after is not None:
                    row_scale(job + 1)
                    norm(job + 1)
                if before == 0:
                    add_ln(job - 1, 2)
                    add_ln(job - 1, 3)
                if layer != after and after is not None:
                    load_mask3()

            jobs(pool, body)
            for p in range(4):
                bias_xe(JOBS - 1, 1, p)


def build_program(nc, a, out):
    N = a["adj"].shape[0]
    B, _, D = a["x"].shape
    x_mid = nc.dram_tensor("x_after_graph_layers", (B, N, D), F32, kind="Internal").ap()
    x_mid2 = nc.dram_tensor("x_after_layer_2", (B, N, D), F32, kind="Internal").ap()
    with ExitStack() as ctx:
        mask = ctx.enter_context(nc.sbuf_tensor("mask", [P, N // P, N], F32))
        shared = [ctx.enter_context(nc.sbuf_tensor(f"shared{i}", [P, N // P, D], F32)) for i in range(2)]
        graph_phase(nc, a, x_mid, mask, shared)
        attention_phase(nc, a, x_mid, x_mid2, out, mask, shared)


_INS = ["x", "adj", "L0_gnn_weight", "L0_gnn_bias", "L1_gnn_weight", "L1_gnn_bias", "L2_gnn_w_qkv",
        "L2_gnn_w_proj", "L2_gnn_b_proj", "L2_gnn_ln_gamma", "L2_gnn_ln_beta", "L3_gnn_Wq", "L3_gnn_bq",
        "L3_gnn_Wk", "L3_gnn_bk", "L3_gnn_Wv", "L3_gnn_bv", "L3_gnn_Wo", "L3_gnn_bo"]


def kernel(**inputs):
    import numpy as _np
    import concourse.bacc as _bacc
    from concourse import mybir as _mybir
    from concourse.bass_utils import run_bass_kernel_spmd as _run

    nc = _bacc.Bacc("TRN2", target_bir_lowering=False, num_devices=1)
    arrays, aps = {}, {}
    for name in _INS:
        arr = _np.ascontiguousarray(inputs[name])
        arrays["in_" + name] = arr
        aps[name] = nc.dram_tensor("in_" + name, arr.shape, _mybir.dt.from_np(arr.dtype), kind="ExternalInput").ap()
    out = nc.dram_tensor("out", inputs["x"].shape, _mybir.dt.float32, kind="ExternalOutput").ap()
    build_program(nc, aps, out)
    r = _run(nc, [arrays], core_ids=[0])
    return r.results[0]["out"]
```
